# Optimizing a Trainium2 kernel written in Bass

```python
import numpy as np
import jax
import jax.numpy as jnp

def _softmax(x, axis=-1):
    return jax.nn.softmax(x, axis=axis)

def _gelu(x):
    return jax.nn.gelu(x, approximate=True)

def _silu(x):
    return jax.nn.silu(x)

def _sigmoid(x):
    return jax.nn.sigmoid(x)

def _layernorm(x, axis=-1, eps=1e-05):
    m = jnp.mean(x, axis=axis, keepdims=True)
    v = jnp.var(x, axis=axis, keepdims=True)
    return (x - m) / jnp.sqrt(v + eps)

def _scatter_add(tgt, idx, src, axis=0):
    return tgt.at[idx].add(src)

def _segment_sum(src, seg, n):
    return jax.ops.segment_sum(src, seg, n)
kernel_name = 'mk_xattn_ffn_d1_seqx_r8_0a059a'

def setup_inputs(seed: int=0):
    np.random.seed(seed)
    _w = jnp.asarray

    def _rec_inputs():
        import jax
        import jax.numpy as jnp
        _rk = jax.random.key(seed)
        x = 4.136e-05 + 0.9999 * jax.random.normal(jax.random.fold_in(_rk, 1), (4, 256, 256), jnp.float32)
        _lenS = 256 - jax.random.randint(jax.random.fold_in(_rk, 7), (4,), 0, max(1, 256 // 4) + 1, jnp.int32)
        _lenS2 = 256 - jax.random.randint(jax.random.fold_in(_rk, 8), (4,), 0, max(1, 256 // 4) + 1, jnp.int32)
        _ctx_1024P = jax.random.normal(jax.random.fold_in(_rk, 11), (4, 16, 128), jnp.float32)
        _ctx_1024c = jax.random.dirichlet(jax.random.fold_in(_rk, 511), 0.3 * jnp.ones((16,), jnp.float32), (4, 256))
        _ctx_1024t = jnp.einsum('bsk,bkd->bsd', _ctx_1024c, _ctx_1024P)
        _ctx_1024t = _ctx_1024t * jax.lax.rsqrt(jnp.mean(jnp.square(_ctx_1024t)) + 1e-12) * 0.953939
        ctx_1024 = -0.000292821 + 1.00034 * (_ctx_1024t + 0.3 * jax.random.normal(jax.random.fold_in(_rk, 611), (4, 256, 128), jnp.float32))
        return (x, ctx_1024)
    x, ctx_1024 = _rec_inputs()

    def _L0_xattn_setup():
        import jax, jax.numpy as jnp
        import numpy as np
        import math
        B, L, DM = (2, 256, 128)
        DS, DC, EXP = (16, 4, 2)
        DI = EXP * DM
        DR = math.ceil(DM / 16)
        DT_MIN, DT_MAX, DT_FLOOR = (0.001, 0.1, 0.0001)

        def _ssm_forward(hidden_states, z, in_proj_w, conv_w, conv_b, x_proj_w, dt_proj_w, dt_proj_b, A_log, D):
            b = hidden_states.shape[0]
            x = jnp.einsum('ed,bld->bel', in_proj_w, hidden_states)
            xp = jnp.pad(x, ((0, 0), (0, 0), (DC - 1, 0)))
            xc = jax.lax.conv_general_dilated(xp, conv_w[:, None, :], window_strides=(1,), padding='VALID', dimension_numbers=('NCH', 'OIH', 'NCH'), feature_group_count=DI)
            u = jax.nn.silu(xc + conv_b[None, :, None])
            x_dbl = jnp.einsum('ke,bel->bkl', x_proj_w, u)
            dt_lo = x_dbl[:, :DR]
            Bm = x_dbl[:, DR:DR + DS]
            Cm = x_dbl[:, DR + DS:]
            delta = jax.nn.softplus(jnp.einsum('er,brl->bel', dt_proj_w, dt_lo) + dt_proj_b[None, :, None])
            A = -jnp.exp(A_log)

            def step(state, xs):
                d_t, B_t, C_t, u_t = xs
                dA = jnp.exp(d_t[..., None] * A)
                state = state * dA + (d_t * u_t)[..., None] * B_t[:, None, :]
                y_t = jnp.einsum('ben,bn->be', state, C_t)
                return (state, y_t)
            xs = (jnp.moveaxis(delta, -1, 0), jnp.moveaxis(Bm, -1, 0), jnp.moveaxis(Cm, -1, 0), jnp.moveaxis(u, -1, 0))
            state0 = jnp.zeros((b, DI, DS), delta.dtype)
            _, ys = jax.lax.scan(step, state0, xs)
            y = jnp.moveaxis(ys, 0, -1)
            y = y + D[None, :, None] * u
            y = y * jax.nn.silu(z)
            return jnp.swapaxes(y, 1, 2)
        key = jax.random.key(seed)
        ks = jax.random.split(key, 8)
        hidden_states = jax.random.normal(ks[0], (B, L, DM), jnp.float32)
        z = jax.random.normal(ks[1], (B, DI, L), jnp.float32)
        in_proj_w = jax.random.normal(ks[2], (DI, DM), jnp.float32) * DM ** (-0.5)
        conv_w = jax.random.normal(ks[3], (DI, DC), jnp.float32) * DC ** (-0.5)
        conv_b = jnp.zeros((DI,), jnp.float32)
        x_proj_w = jax.random.normal(ks[4], (DR + 2 * DS, DI), jnp.float32) * DI ** (-0.5)
        dt_std = DR ** (-0.5)
        dt_proj_w = jax.random.uniform(ks[5], (DI, DR), jnp.float32, -dt_std, dt_std)
        dt = jnp.exp(jax.random.uniform(ks[6], (DI,), jnp.float32) * (math.log(DT_MAX) - math.log(DT_MIN)) + math.log(DT_MIN))
        dt = jnp.clip(dt, DT_FLOOR)
        dt_proj_b = dt + jnp.log(-jnp.expm1(-dt))
        A_log = jnp.log(jnp.broadcast_to(jnp.arange(1, DS + 1, dtype=jnp.float32), (DI, DS)))
        D = jnp.ones((DI,), jnp.float32)
        return dict(hidden_states=hidden_states, z=z, in_proj_w=in_proj_w, conv_w=conv_w, conv_b=conv_b, x_proj_w=x_proj_w, dt_proj_w=dt_proj_w, dt_proj_b=dt_proj_b, A_log=A_log, D=D)
    _L0_xattn_all = _L0_xattn_setup()
    _L0_xattn_in = {k: v for k, v in _L0_xattn_all.items() if k in ('in_proj_w', 'conv_w', 'conv_b', 'x_proj_w', 'dt_proj_w', 'dt_proj_b', 'A_log', 'D')}
    del _L0_xattn_all

    def _L0_ffn_setup():
        import jax, jax.numpy as jnp
        import numpy as np
        import math
        D_MODEL = 256
        D_FF = 1024
        NUM_EXPERTS = 8
        TOP_K = 2
        CAPACITY_FACTOR = 1.25
        BATCH, SEQ = (4, 256)

        def _moe_forward(x, Wg, w1, w2):
            B, T, d = x.shape
            S = B * T
            E, K = (NUM_EXPERTS, TOP_K)
            C = math.ceil(CAPACITY_FACTOR * S * K / E)
            xr = x.reshape(S, d)
            probs = jax.nn.softmax(xr @ Wg, axis=-1)
            gate_vals, expert_idx = jax.lax.top_k(probs, K)
            flat_e = expert_idx.reshape(-1)
            oh = jax.nn.one_hot(flat_e, E, dtype=jnp.int32)
            pos = jnp.sum((jnp.cumsum(oh, axis=0) - 1) * oh, axis=1)
            kept = pos < C
            i = jnp.arange(S * K)
            slot = i % K * S + i // K
            sentinel = S * K
            pos_w = jnp.where(kept, pos, C)
            dispatch_mask = jnp.full((E, C), sentinel, dtype=jnp.int32)
            dispatch_mask = dispatch_mask.at[flat_e, pos_w].set(slot.astype(jnp.int32), mode='drop')
            combine_weights = (gate_vals * kept.reshape(S, K)).T
            dispatched = xr[dispatch_mask.reshape(-1) % S].reshape(E, C, d)
            h = jax.nn.relu(jnp.einsum('ecd,edf->ecf', dispatched, w1))
            expert_out = jnp.einsum('ecf,efd->ecd', h, w2)
            rerouted = jnp.zeros((S * K + 1, d), dtype=expert_out.dtype)
            rerouted = rerouted.at[dispatch_mask.reshape(-1)].set(expert_out.reshape(-1, d))
            rerouted = rerouted[:-1].reshape(K, S, d)
            out = jnp.einsum('ks,ksm->sm', combine_weights, rerouted)
            return out.reshape(B, T, d)
        key = jax.random.key(seed)
        k1, k2, k3, k4 = jax.random.split(key, 4)
        x = jax.random.normal(k1, (BATCH, SEQ, D_MODEL), dtype=jnp.float32)
        Wg = jax.random.normal(k2, (D_MODEL, NUM_EXPERTS), dtype=jnp.float32) * 0.02
        w1 = jax.random.normal(k3, (NUM_EXPERTS, D_MODEL, D_FF), dtype=jnp.float32) * 0.02
        w2 = jax.random.normal(k4, (NUM_EXPERTS, D_FF, D_MODEL), dtype=jnp.float32) * 0.02
        return {'x': x, 'Wg': Wg, 'w1': w1, 'w2': w2}
    _L0_ffn_all = _L0_ffn_setup()
    _L0_ffn_in = {k: v for k, v in _L0_ffn_all.items() if k in ('Wg', 'w1', 'w2')}
    del _L0_ffn_all
    return {'x': x, 'ctx_1024': ctx_1024, 'L0_xattn_in_proj_w': _L0_xattn_in['in_proj_w'], 'L0_xattn_conv_w': _L0_xattn_in['conv_w'], 'L0_xattn_conv_b': _L0_xattn_in['conv_b'], 'L0_xattn_x_proj_w': _L0_xattn_in['x_proj_w'], 'L0_xattn_dt_proj_w': _L0_xattn_in['dt_proj_w'], 'L0_xattn_dt_proj_b': _L0_xattn_in['dt_proj_b'], 'L0_xattn_A_log': _L0_xattn_in['A_log'], 'L0_xattn_D': _L0_xattn_in['D'], 'L0_ffn_Wg': _L0_ffn_in['Wg'], 'L0_ffn_w1': _L0_ffn_in['w1'], 'L0_ffn_w2': _L0_ffn_in['w2']}

def reference(x, ctx_1024, L0_xattn_in_proj_w, L0_xattn_conv_w, L0_xattn_conv_b, L0_xattn_x_proj_w, L0_xattn_dt_proj_w, L0_xattn_dt_proj_b, L0_xattn_A_log, L0_xattn_D, L0_ffn_Wg, L0_ffn_w1, L0_ffn_w2):
    import jax
    import jax.numpy as jnp

    def _L0_xattn_ref(hidden_states, z, in_proj_w, conv_w, conv_b, x_proj_w, dt_proj_w, dt_proj_b, A_log, D):
        import jax, jax.numpy as jnp
        import numpy as np
        import math
        B, L, DM = (2, 256, 128)
        DS, DC, EXP = (16, 4, 2)
        DI = EXP * DM
        DR = math.ceil(DM / 16)
        DT_MIN, DT_MAX, DT_FLOOR = (0.001, 0.1, 0.0001)

        def _ssm_forward(hidden_states, z, in_proj_w, conv_w, conv_b, x_proj_w, dt_proj_w, dt_proj_b, A_log, D):
            b = hidden_states.shape[0]
            x = jnp.einsum('ed,bld->bel', in_proj_w, hidden_states)
            xp = jnp.pad(x, ((0, 0), (0, 0), (DC - 1, 0)))
            xc = jax.lax.conv_general_dilated(xp, conv_w[:, None, :], window_strides=(1,), padding='VALID', dimension_numbers=('NCH', 'OIH', 'NCH'), feature_group_count=DI)
            u = jax.nn.silu(xc + conv_b[None, :, None])
            x_dbl = jnp.einsum('ke,bel->bkl', x_proj_w, u)
            dt_lo = x_dbl[:, :DR]
            Bm = x_dbl[:, DR:DR + DS]
            Cm = x_dbl[:, DR + DS:]
            delta = jax.nn.softplus(jnp.einsum('er,brl->bel', dt_proj_w, dt_lo) + dt_proj_b[None, :, None])
            A = -jnp.exp(A_log)

            def step(state, xs):
                d_t, B_t, C_t, u_t = xs
                dA = jnp.exp(d_t[..., None] * A)
                state = state * dA + (d_t * u_t)[..., None] * B_t[:, None, :]
                y_t = jnp.einsum('ben,bn->be', state, C_t)
                return (state, y_t)
            xs = (jnp.moveaxis(delta, -1, 0), jnp.moveaxis(Bm, -1, 0), jnp.moveaxis(Cm, -1, 0), jnp.moveaxis(u, -1, 0))
            state0 = jnp.zeros((b, DI, DS), delta.dtype)
            _, ys = jax.lax.scan(step, state0, xs)
            y = jnp.moveaxis(ys, 0, -1)
            y = y + D[None, :, None] * u
            y = y * jax.nn.silu(z)
            return jnp.swapaxes(y, 1, 2)
        return _ssm_forward(hidden_states, z, in_proj_w, conv_w, conv_b, x_proj_w, dt_proj_w, dt_proj_b, A_log, D)

    def _L0_ffn_ref(x, Wg, w1, w2):
        import jax, jax.numpy as jnp
        import numpy as np
        import math
        D_MODEL = 256
        D_FF = 1024
        NUM_EXPERTS = 8
        TOP_K = 2
        CAPACITY_FACTOR = 1.25
        BATCH, SEQ = (4, 256)

        def _moe_forward(x, Wg, w1, w2):
            B, T, d = x.shape
            S = B * T
            E, K = (NUM_EXPERTS, TOP_K)
            C = math.ceil(CAPACITY_FACTOR * S * K / E)
            xr = x.reshape(S, d)
            probs = jax.nn.softmax(xr @ Wg, axis=-1)
            gate_vals, expert_idx = jax.lax.top_k(probs, K)
            flat_e = expert_idx.reshape(-1)
            oh = jax.nn.one_hot(flat_e, E, dtype=jnp.int32)
            pos = jnp.sum((jnp.cumsum(oh, axis=0) - 1) * oh, axis=1)
            kept = pos < C
            i = jnp.arange(S * K)
            slot = i % K * S + i // K
            sentinel = S * K
            pos_w = jnp.where(kept, pos, C)
            dispatch_mask = jnp.full((E, C), sentinel, dtype=jnp.int32)
            dispatch_mask = dispatch_mask.at[flat_e, pos_w].set(slot.astype(jnp.int32), mode='drop')
            combine_weights = (gate_vals * kept.reshape(S, K)).T
            dispatched = xr[dispatch_mask.reshape(-1) % S].reshape(E, C, d)
            h = jax.nn.relu(jnp.einsum('ecd,edf->ecf', dispatched, w1))
            expert_out = jnp.einsum('ecf,efd->ecd', h, w2)
            rerouted = jnp.zeros((S * K + 1, d), dtype=expert_out.dtype)
            rerouted = rerouted.at[dispatch_mask.reshape(-1)].set(expert_out.reshape(-1, d))
            rerouted = rerouted[:-1].reshape(K, S, d)
            out = jnp.einsum('ks,ksm->sm', combine_weights, rerouted)
            return out.reshape(B, T, d)
        return _moe_forward(x, Wg, w1, w2)
    x = x + _L0_xattn_ref(ctx_1024, _layernorm(x, axis=-1), L0_xattn_in_proj_w, L0_xattn_conv_w, L0_xattn_conv_b, L0_xattn_x_proj_w, L0_xattn_dt_proj_w, L0_xattn_dt_proj_b, L0_xattn_A_log, L0_xattn_D)
    x = x + _L0_ffn_ref(_layernorm(x, axis=-1), L0_ffn_Wg, L0_ffn_w1, L0_ffn_w2)
    return x

_drawn_inputs = setup_inputs


def setup_inputs(seed=0):
    import zlib

    import numpy as np

    out = dict(_drawn_inputs(seed))
    spreads = {'L0_xattn_conv_b': (0.0, 0.1), 'L0_xattn_D': (1.0, 0.2)}
    factors = {'L0_xattn_dt_proj_w': 6.066}
    for name, (base, spread) in spreads.items():
        noise = np.random.default_rng([zlib.crc32(name.encode()), seed]).standard_normal(out[name].shape)
        drawn = base * np.exp(spread * noise) if base else spread * noise
        out[name] = jnp.asarray(drawn.astype(out[name].dtype))
    for name, factor in factors.items():
        out[name] = (out[name] * factor).astype(out[name].dtype)
    return out
```

```python
from contextlib import ExitStack

import numpy as np

import concourse.bass as bass
from concourse import mybir

F32 = mybir.dt.float32
BF16 = mybir.dt.bfloat16
U32 = mybir.dt.uint32
ALU = mybir.AluOpType
ACT = mybir.ActivationFunctionType
AX = mybir.AxisListType

P = 128
B, L, DM = 4, 256, 256
DC = 128
DI, DS, TAPS, DR = 256, 16, 4, 8
EC = DI // P
T = B * L
TILES = T // P
HALVES = 2
HT = T // HALVES
HTILES = HT // P
HB = B // HALVES
NE, TOPK, DFF = 8, 2, 1024
CAP = (5 * T * TOPK // NE + 3) // 4
SLOTS = NE * CAP
STILES = SLOTS // P
PAIRS = NE // 2
PTILES = STILES // PAIRS
FC = DFF // P
KC = DM // P
ROW = DM + 2
NROWS = T * TOPK
DROPPED = 8192.0
EPS = 1e-5
CW, CB, DTB, DSK, ALOG, NCH = 0, TAPS, TAPS + 1, TAPS + 2, TAPS + 3, TAPS + 3 + DS
CID, CTRI, CDST = 0, P, 2 * P
CBASE = CDST + TILES * TOPK
CIOTA = CBASE + NE
NCONST = CIOTA + NE
BC = 2 * DS
XPC = DR + 3 * BC
ARENA = 26000


def build(nc, x, ctx_t, inproj_t, xproj_t, dtproj_t, chan, wg, w1, w2, consts, sel, out):
    xe_dram = nc.dram_tensor("expert_rows", [SLOTS, ROW], F32, kind="Internal").ap()
    res_dram = nc.dram_tensor("result_rows", [NROWS, DM], F32, kind="Internal").ap()

    with ExitStack() as ctx:
        def sb(name, shape, dt=F32):
            return ctx.enter_context(nc.sbuf_tensor(name, shape, dt))

        def sem(name):
            return ctx.enter_context(nc.semaphore(name))

        cst = sb("cst", [P, NCONST])
        ident = cst[:, CID:CID + P]
        ch = sb("ch", [P, EC, NCH])
        xnat = sb("xnat", [P, TILES, DM])
        x1 = sb("x1", [P, TILES, DM])
        xrow = sb("xrow", [P, TILES, TOPK, ROW])
        zst = sb("zst", [P, TILES, DM])
        wgs = sb("wgs", [P, KC, NE])
        w1s = [sb(f"w1s{s}", [P, KC, DFF]) for s in range(2)]
        w2s = [sb(f"w2s{s}", [P, FC, DM]) for s in range(2)]
        anegs = sb("anegs", [P, EC, DS])
        diagd = sb("diagd", [P, EC, P])
        tri = sb("tri", [P, P], BF16)
        ones = sb("ones", [P, P], BF16)
        fill = sb("fill", [P, ROW])
        epst = sb("epst", [P, 1])
        nhalf = sb("nhalf", [P, TILES])
        stats = sb("stats", [P, TILES, 6])
        mvz = sb("mvz", [P, TILES, 2])
        mvx = sb("mvx", [P, TILES, 2])
        rstd = sb("rstd", [P, TILES])
        nmr = sb("nmr", [P, TILES])
        rx = sb("rx", [P, TILES])
        rv = sb("rv", [P, TILES])
        lg = sb("lg", [P, TILES, NE])
        rmax = sb("rmax", [P, TILES])
        rsum = sb("rsum", [P, TILES])
        top = sb("top", [P, TILES, NE])
        topi = sb("topi", [P, TILES, NE], U32)
        topf = sb("topf", [P, TILES, TOPK])
        oh = sb("oh", [P, TILES, TOPK, NE])
        ohc = sb("ohc", [P, TILES, TOPK, NE])
        multi = sb("multi", [P, TILES, NE], BF16)
        pos = sb("pos", [P, TILES, TOPK])
        slot = sb("slot", [P, TILES, TOPK])
        sloti = sb("sloti", [P, TILES, TOPK], U32)
        arena = sb("arena", [P, ARENA])
        at = [0]

        def carve(shape, dt=F32, parts=P):
            n = int(np.prod(shape)) * (2 if dt == BF16 else 4) // 4
            a = arena[0:parts, at[0]:at[0] + n]
            at[0] += n
            assert at[0] <= ARENA, at[0]
            if dt != F32:
                a = a.bitcast(dt)
            if len(shape) == 2:
                a = a.rearrange("p (a b) -> p a b", a=shape[0])
            if len(shape) == 3:
                a = a.rearrange("p (a b c) -> p a b c", a=shape[0], b=shape[1])
            return a

        ctxs = carve([T])
        inps = carve([DI])
        xps = carve([EC, XPC])
        dtps = carve([DI], parts=DR)
        dtlo = carve([T], parts=DR)
        zs = carve([TILES, DM])
        u = carve([EC, T])
        delta = carve([EC, T])
        du = carve([EC, T])
        sels = carve([2 * DS * P], BF16, parts=3 * BC)
        stack = carve([T], BF16, parts=3 * BC)
        rest = carve([HT], parts=3 * BC)
        bsb = [carve([HT]) for _ in range(2)]
        dbu = [carve([EC, HT]) for _ in range(2)]
        h = [carve([EC, HT]) for _ in range(2)]
        hc = [carve([EC, HT]) for _ in range(2)]
        conv = [h[0], h[1]]
        spe = [hc[0], hc[1]]
        spl = [dbu[0], dbu[1]]
        spr = [carve([EC, HT]) for _ in range(HALVES)]
        xnt = carve([KC, HT])
        at[0] = 0
        xe = carve([STILES, ROW])
        xt = carve([KC, SLOTS])
        ht = [carve([FC, CAP]) for _ in range(2)]
        eot = carve([KC, 2 * CAP])
        eo = carve([PTILES, DM])
        at[0] = 0
        resl = carve([TOPK, TILES, DM])
        dst = sb("dst", [P, PTILES], U32)

        ps = ctx.enter_context(nc.psum_tensor("ps", [P, 8, HT], F32))
        y = ps[:, 0:2, :].rearrange("p b (t e) -> p (b t) e", e=DI)
        da = [ps[:, 2:4, :], ps[:, 4:6, :]]
        cps = ps[:, 6, :]
        bps = ps[:, 7, :]

        s = {n: sem(n) for n in (
            "x_in ctx_in small_in sel_in w_in0 w_in1 fill_made xe_filled res_filled "
            "xe_in0 xe_in1 xe_in2 xe_in3 "
            "z_stats z_rstd z_scale zs_done zt_psum zt_done "
            "xin_psum conv_first conv_done u_done bc_psum dtlo_psum dtlo_done hi_done stack_done "
            "dt_psum sp_exp sp_relu sp_ln delta_done du_done a_done "
            "b_psum b_done c_psum da_done scan_done dbu_done mult_done ysum_done "
            "x1_done ln_rstd ln_var xn_done xt_psum xt_done lg_psum lg_sub lg_exp multi_done "
            "pos_psum slots_done scattered xt2_psum xt2_act xt2_dve "
            "h_psum h_act h_dve o_psum o_done t_psum t_act t_dve dst_done res_out "
            "res_in0 res_in1 res_in2 res_in3 sum_done out_done "
            "dve_step act_step").split()}

        block = ctx.enter_context(nc.Block())

        @block.sync
        def _(sp):
            sp.dma_start(ctxs, ctx_t).then_inc(s["ctx_in"], 16)
            sp.dma_start(inps, inproj_t).then_inc(s["ctx_in"], 16)
            sp.dma_start(ch[:], chan).then_inc(s["small_in"], 16)
            sp.dma_start(xps, xproj_t).then_inc(s["small_in"], 16)
            sp.dma_start(dtps, dtproj_t).then_inc(s["small_in"], 16)
            sp.dma_start(cst[:], consts).then_inc(s["small_in"], 16)
            sp.dma_start(wgs[:], wg).then_inc(s["small_in"], 16)
            sp.dma_start(xnat[:], x).then_inc(s["x_in"], 16)
            sp.dma_start(sels, sel).then_inc(s["sel_in"], 16)
            for e in range(2):
                sp.dma_start(w1s[e][:], w1[e]).then_inc(s[f"w_in{e}"], 16)
                sp.dma_start(w2s[e][:], w2[e]).then_inc(s[f"w_in{e}"], 16)
            sp.wait_ge(s["fill_made"], 1)
            sp.dma_start(xe_dram.rearrange("(t p) r -> p t r", p=P),
                         fill[:, None, :].to_broadcast([P, STILES, ROW])).then_inc(s["xe_filled"], 16)
            sp.dma_start(res_dram.rearrange("(t p) r -> p t r", p=P),
                         fill[:, None, 0:DM].to_broadcast([P, NROWS // P, DM])).then_inc(s["res_filled"], 16)
            sp.wait_ge(s["scattered"], 16 * TILES * TOPK)
            for q in range(PAIRS):
                tiles = slice(q * PTILES, (q + 1) * PTILES)
                sp.dma_start(xe[:, tiles, :],
                             xe_dram.rearrange("(t p) r -> p t r", p=P)[:, tiles, :]).then_inc(s[f"xe_in{q}"], 16)
            with sp.Fori(1, PAIRS) as q:
                for e in range(2):
                    sp.wait_ge(s["o_psum"], 2 * q - 1 + e)
                    sp.dma_start(w1s[e][:], w1[bass.ds(2 * q + e, 1)].rearrange("o p k f -> p (o k) f")
                                 ).then_inc(s[f"w_in{e}"], 16)
                    sp.dma_start(w2s[e][:], w2[bass.ds(2 * q + e, 1)].rearrange("o p k f -> p (o k) f")
                                 ).then_inc(s[f"w_in{e}"], 16)
            sp.wait_ge(s["res_out"], 16 * STILES)
            for q in range(4):
                for k in range(TOPK):
                    rows = res_dram[k * T + q * 2 * P:k * T + (q + 1) * 2 * P]
                    sp.dma_start(resl[:, k, 2 * q:2 * q + 2, :],
                                 rows.rearrange("(t p) d -> p t d", p=P)).then_inc(s[f"res_in{q}"], 16)
            for q in range(4):
                sp.wait_ge(s["sum_done"], q + 1)
                sp.dma_start(out[q * 2 * P:(q + 1) * 2 * P].rearrange("(t p) d -> p t d", p=P),
                             x1[:, 2 * q:2 * q + 2, :]).then_inc(s["out_done"], 16)
            sp.wait_ge(s["out_done"], 64)

        @block.gpsimd
        def _(pool):
            nc.gpsimd.memset(fill[:, 0:DM + 1], 0.0)
            nc.gpsimd.memset(ones[:], 1.0)
            nc.gpsimd.memset(nhalf[:], -0.5)
            nc.gpsimd.memset(epst[:], EPS)
            nc.gpsimd.memset(fill[:, DM + 1:ROW], DROPPED).then_inc(s["fill_made"], 1)
            pool.sem_inc(s["dbu_done"], 2)
            pool.wait_ge(s["z_stats"], 1)
            pool.wait_ge(s["fill_made"], 1)
            nc.gpsimd.tensor_tensor(rstd[:], rv[:], nhalf[:], ALU.pow).then_inc(s["z_rstd"], 1)
            for hb in range(HALVES):
                cols = slice(hb * HT, (hb + 1) * HT)
                pool.wait_ge(s["delta_done"], 2 * (hb + 1))
                nc.gpsimd.tensor_tensor(du[:, :, cols], delta[:, :, cols], u[:, :, cols],
                                        ALU.mult).then_inc(s["du_done"], 1)

            def step(hb, g, par):
                pool.wait_ge(s["b_done"], g + 1)
                pool.wait_ge(s["scan_done"], g + 1)
                nc.gpsimd.tensor_tensor(dbu[par], du[:, :, hb * HT:(hb + 1) * HT],
                                        bsb[par][:, None, :].to_broadcast([P, EC, HT]), ALU.mult
                                        ).then_inc(s["dbu_done"], 1)

            pool.wait_ge(s["du_done"], 2)
            pool.wait_ge(s["delta_done"], 4)
            for hb in range(HALVES):
                with pool.Fori(0, DS // 2) as i:
                    for par in range(2):
                        step(hb, hb * DS + 2 * i + par, par)
            pool.wait_ge(s["xe_filled"], 16)
            for hb in range(HALVES):
                tiles = slice(hb * HTILES, (hb + 1) * HTILES)
                pool.wait_ge(s["ln_var"], hb + 1)
                nc.gpsimd.tensor_tensor(rx[:, tiles], rv[:, tiles], nhalf[:, tiles], ALU.pow
                                        ).then_inc(s["ln_rstd"], 1)
                pool.wait_ge(s["slots_done"], hb + 1)
                for j in range(hb * HTILES, (hb + 1) * HTILES):
                    for k in range(TOPK):
                        nc.gpsimd.indirect_dma_start(
                            xe_dram, bass.IndirectOffsetOnAxis(ap=sloti[:, j, k:k + 1], axis=0),
                            xrow[:, j, k, :], None, bounds_check=SLOTS - 1, oob_is_err=False
                        ).then_inc(s["scattered"], 16)
            pool.wait_ge(s["res_filled"], 16)
            last_row = pool.to_reg(NROWS - 1)
            for q in range(PAIRS):
                pool.wait_ge(s["dst_done"], q + 1)
                for t in range(PTILES):
                    if t % 2 == 0:
                        pool.wait_ge(s["t_act"], 3 * q + t // 2 + 1)
                    else:
                        pool.wait_ge(s["t_dve"], 2 * q + t // 2 + 1)
                    nc.gpsimd.indirect_dma_start(
                        res_dram, bass.IndirectOffsetOnAxis(ap=dst[:, t:t + 1], axis=0),
                        eo[:, t, :], None, bounds_check=last_row, oob_is_err=False
                    ).then_inc(s["res_out"], 16)

        @block.scalar
        def _(act):
            act.wait_ge(s["small_in"], 80)
            act.wait_ge(s["x_in"], 16)
            for hb in range(HALVES):
                for c in range(EC):
                    act.wait_ge(s["xin_psum"], hb * EC + c + 1)
                    nc.scalar.activation(conv[hb][:, c, :], ps[:, 2 + hb * EC + c, :], ACT.Identity,
                                         bias=ch[:, c, CB:CB + 1], scale=ch[:, c, CW + TAPS - 1:CW + TAPS]
                                         ).then_inc(s["conv_first"], 1)
            for hb in range(HALVES):
                for c in range(EC):
                    act.wait_ge(s["conv_done"], hb * EC + c + 1)
                    nc.scalar.activation(u[:, c, hb * HT:(hb + 1) * HT], conv[hb][:, c, :], ACT.Silu
                                         ).then_inc(s["u_done"], 1)
            act.wait_ge(s["z_scale"], 1)
            for j in range(TILES):
                ins = nc.scalar.activation(zs[:, j, :], xnat[:, j, :], ACT.Silu,
                                           bias=nmr[:, j:j + 1], scale=rstd[:, j:j + 1])
            ins.then_inc(s["zs_done"], 1)
            for hb in range(HALVES):
                cols = slice(hb * HT, (hb + 1) * HT)
                act.wait_ge(s["dtlo_psum"], hb + 1)
                nc.scalar.activation(dtlo[:, cols], ps[0:DR, hb, :], ACT.Copy).then_inc(s["dtlo_done"], 1)
                act.wait_ge(s["bc_psum"], hb + 1)
                nc.scalar.activation(stack[:, cols], ps[0:3 * BC, 6 + hb, :], ACT.Copy
                                     ).then_inc(s["hi_done"], 1)
            nc.scalar.activation(anegs[:], ch[:, :, ALOG:ALOG + DS], ACT.Exp).then_inc(s["act_step"], 1)
            for hb in range(HALVES):
                for c in range(EC):
                    q = hb * EC + c
                    v = ps[:, 2 + q, :]
                    act.wait_ge(s["dt_psum"], q + 1)
                    nc.scalar.activation(spe[hb][:, c, :], v, ACT.Abs, bias=ch[:, c, DTB:DTB + 1]
                                         ).then_inc(s["act_step"], 1)
                    nc.scalar.activation(spr[hb][:, c, :], v, ACT.Relu, bias=ch[:, c, DTB:DTB + 1]
                                         ).then_inc(s["sp_relu"], 1)
                    act.wait_ge(s["act_step"], q + 2)
                    nc.scalar.activation(spe[hb][:, c, :], spe[hb][:, c, :], ACT.Exp, scale=-1.0
                                         ).then_inc(s["sp_exp"], 1)
            for hb in range(HALVES):
                for c in range(EC):
                    act.wait_ge(s["sp_exp"], hb * EC + c + 1)
                    nc.scalar.activation(spl[hb][:, c, :], spe[hb][:, c, :], ACT.Ln, bias=1.0
                                         ).then_inc(s["sp_ln"], 1)

            def b_copy(g, par):
                act.wait_ge(s["b_psum"], g + 1)
                act.wait_ge(s["dbu_done"], g + 1)
                nc.scalar.activation(bsb[par], bps, ACT.Copy).then_inc(s["b_done"], 1)

            def decay(hb, g, n, par):
                act.wait_ge(s["scan_done"], g + 1)
                for c in range(EC):
                    cols = delta[:, c, hb * HT:(hb + 1) * HT].rearrange("p (b l) -> p b l", b=HB)
                    nc.scalar.activation(
                        da[par][:, c, :].rearrange("p (b l) -> p b l", b=HB)[:, :, 1:L], cols[:, :, 1:L],
                        ACT.Exp, scale=anegs[:, c, n:n + 1]).then_inc(s["da_done"], 1)

            act.wait_ge(s["delta_done"], 4)
            act.wait_ge(s["a_done"], 1)
            b_copy(0, 0)
            for g in range(HALVES * DS):
                decay(g // DS, g, g % DS, g % 2)
                if g + 1 < HALVES * DS:
                    b_copy(g + 1, 1 - g % 2)

            for hb in range(HALVES):
                tiles = slice(hb * HTILES, (hb + 1) * HTILES)
                act.wait_ge(s["xt_psum"], hb + 1)
                for c in range(KC):
                    nc.scalar.activation(xnt[:, c, :], ps[:, 2 + c, :], ACT.Copy).then_inc(s["xt_done"], 1)
                act.wait_ge(s["lg_sub"], hb + 1)
                nc.scalar.activation(lg[:, tiles, :], lg[:, tiles, :], ACT.Exp).then_inc(s["lg_exp"], 1)

            for m in range(0, STILES // 2, 2):
                act.wait_ge(s["xt2_psum"], m + 1)
                nc.scalar.activation(
                    xt[:, :, 2 * m * P:(2 * m + 2) * P].rearrange("p c (t n) -> p c t n", n=P),
                    ps[:, m % 4, :].rearrange("p (t c n) -> p c t n", t=2, c=KC), ACT.Copy
                ).then_inc(s["xt2_act"], 1)
            with act.Fori(0, PAIRS) as q:
                for e in range(2):
                    for f in range(0, FC, 2):
                        n = (2 * q + e) * FC + f
                        act.wait_ge(s["h_psum"], n + 1)
                        nc.scalar.activation(ht[e][:, f, :], ps[:, f % 4, 0:CAP], ACT.Relu
                                             ).then_inc(s["h_act"], 1)
                    act.wait_ge(s["o_psum"], 2 * q + e + 1)
                    nc.scalar.activation(eot[:, :, e * CAP:(e + 1) * CAP], ps[:, 4:6, 0:CAP], ACT.Copy
                                         ).then_inc(s["o_done"], 1)
                for t in range(0, PTILES, 2):
                    act.wait_ge(s["t_psum"], q * PTILES + t + 1)
                    act.wait_ge(s["res_out"], 16 * PTILES * q)
                    nc.scalar.activation(eo[:, t, :], ps[:, 6 + t % 2, 0:DM], ACT.Copy,
                                         scale=xe[:, bass.ds(q * PTILES + t, 1), DM:DM + 1]
                                         .rearrange("p a b -> p (a b)")).then_inc(s["t_act"], 1)

        @block.tensor
        def _(pe):
            pe.sem_inc(s["ysum_done"], 2)
            pe.wait_ge(s["ctx_in"], 32)
            for hb in range(HALVES):
                for c in range(EC):
                    nc.tensor.matmul(ps[:, 2 + hb * EC + c, :], inps[:, c * P:(c + 1) * P],
                                     ctxs[:, hb * HT:(hb + 1) * HT], start=True, stop=True
                                     ).then_inc(s["xin_psum"], 1)
            pe.wait_ge(s["small_in"], 80)
            for hb in range(HALVES):
                cols = slice(hb * HT, (hb + 1) * HT)
                pe.wait_ge(s["u_done"], EC * (hb + 1))
                for c in range(EC):
                    ins = nc.tensor.matmul(ps[0:DR, hb, :], xps[:, c, 0:DR], u[:, c, cols],
                                           start=(c == 0), stop=(c == EC - 1))
                ins.then_inc(s["dtlo_psum"], 1)
                for c in range(EC):
                    ins = nc.tensor.matmul(ps[0:3 * BC, 6 + hb, :], xps[:, c, DR:XPC], u[:, c, cols],
                                           start=(c == 0), stop=(c == EC - 1))
                ins.then_inc(s["bc_psum"], 1)
            for hb in range(HALVES):
                pe.wait_ge(s["dtlo_done"], hb + 1)
                for c in range(EC):
                    nc.tensor.matmul(ps[:, 2 + hb * EC + c, :], dtps[:, c * P:(c + 1) * P],
                                     dtlo[:, hb * HT:(hb + 1) * HT], start=True, stop=True
                                     ).then_inc(s["dt_psum"], 1)
            def z_turn(m):
                for n in range(4):
                    j, c = 2 * m + n // 2, n % 2
                    ins = nc.tensor.transpose(
                        ps[:, m % 2, n * P:(n + 1) * P],
                        zs[:, (j // 2) * 2 + c, (j % 2) * P:(j % 2 + 1) * P], ident)
                ins.then_inc(s["zt_psum"], 1)

            def b_cast(hb, g, n):
                pe.wait_ge(s["b_done"], g)
                nc.tensor.matmul(bps, sels[:, bass.ds(n * P, P)], stack[:, hb * HT:(hb + 1) * HT],
                                 start=True, stop=True).then_inc(s["b_psum"], 1)

            def c_cast(hb, g, n):
                pe.wait_ge(s["mult_done"], g + 2)
                nc.tensor.matmul(cps, sels[:, bass.ds((DS + n) * P, P)], stack[:, hb * HT:(hb + 1) * HT],
                                 start=True, stop=True).then_inc(s["c_psum"], 1)

            def state_sum(g, par, last=False):
                pe.wait_ge(s["mult_done"], g + 3)
                for t in range(HTILES):
                    for c in range(EC):
                        ins = nc.tensor.matmul(y[:, t, c * P:(c + 1) * P], hc[par][:, c, t * P:(t + 1) * P],
                                               ident, start=False, stop=last, skip_group_check=True)
                ins.then_inc(s["ysum_done"], 1)

            pe.wait_ge(s["sel_in"], 16)
            pe.wait_ge(s["stack_done"], 2)
            b_cast(0, 0, 0)
            pe.wait_ge(s["zs_done"], 1)
            z_turn(0)
            z_turn(1)
            b_cast(0, 1, 1)
            for m in (2, 3):
                pe.wait_ge(s["zt_done"], m - 1)
                z_turn(m)
            for hb in range(HALVES):
                pe.wait_ge(s["a_done"], 2)
                if hb == 0:
                    pe.wait_ge(s["zt_done"], 4)
                else:
                    pe.wait_ge(s["x1_done"], 1)
                for t in range(HTILES):
                    for c in range(EC):
                        nc.tensor.matmul(y[:, t, c * P:(c + 1) * P],
                                         u[:, c, hb * HT + t * P:hb * HT + (t + 1) * P], diagd[:, c, :],
                                         start=(t % 2 == 0 and c == 0), stop=False, skip_group_check=True)
                for n in range(2):
                    b_cast(hb, hb * DS + n + 2, n + 2)
                    c_cast(hb, hb * DS + n, n)
                    if n:
                        state_sum(hb * DS + n - 1, 1 - n)
                with pe.Fori(1, DS // 2 - 1) as i:
                    for par in range(2):
                        g = hb * DS + 2 * i + par
                        b_cast(hb, g + 2, 2 * i + par + 2)
                        c_cast(hb, g, 2 * i + par)
                        state_sum(g - 1, 1 - par)
                for n in (DS - 2, DS - 1):
                    if hb + 1 < HALVES:
                        b_cast(hb + 1, hb * DS + n + 2, n + 2 - DS)
                    c_cast(hb, hb * DS + n, n)
                    state_sum(hb * DS + n - 1, 1 - n % 2)
                state_sum(hb * DS + DS - 1, 1, last=True)

            for hb in range(HALVES):
                pe.wait_ge(s["xn_done"], hb + 1)
                for c in range(KC):
                    for t in range(HTILES):
                        ins = nc.tensor.transpose(ps[:, 2 + c, t * P:(t + 1) * P],
                                                  xrow[:, hb * HTILES + t, 0, c * P:(c + 1) * P], ident)
                ins.then_inc(s["xt_psum"], 1)
                pe.wait_ge(s["xt_done"], KC * (hb + 1))
                for t in range(HTILES):
                    for c in range(KC):
                        ins = nc.tensor.matmul(ps[:, 4, t * NE:(t + 1) * NE], xnt[:, c, t * P:(t + 1) * P],
                                               wgs[:, c, :], start=(t == 0 and c == 0), stop=(c == KC - 1),
                                               skip_group_check=True)
                ins.then_inc(s["lg_psum"], 1)
                pe.wait_ge(s["multi_done"], hb + 1)
                cum = ps[:, 5, 0:HTILES * NE].rearrange("p (t e) -> p t e", e=NE)
                mh = multi[:, hb * HTILES:(hb + 1) * HTILES, :]
                last = nc.tensor.matmul(cum, tri[:], mh, start=True, stop=False, skip_group_check=True)
                for t in range(1, HTILES):
                    last = nc.tensor.matmul(cum[:, t:HTILES, :], ones[:], mh[:, 0:HTILES - t, :], start=False,
                                            stop=False, skip_group_check=True)
                for j in range(hb * HTILES):
                    last = nc.tensor.matmul(cum, ones[:], multi[:, j:j + 1, :].to_broadcast([P, HTILES, NE]),
                                            start=False, stop=False, skip_group_check=True)
                last.then_inc(s["pos_psum"], 1)

            for m in range(STILES // 2):
                for q in {2 * m // PTILES, (2 * m + 1) // PTILES}:
                    pe.wait_ge(s[f"xe_in{q}"], 16)
                if m >= 4:
                    pe.wait_ge(s["xt2_act" if m % 2 == 0 else "xt2_dve"], (m - 4) // 2 + 1)
                for t in range(2):
                    for c in range(KC):
                        ins = nc.tensor.transpose(ps[:, m % 4, (t * KC + c) * P:(t * KC + c + 1) * P],
                                                  xe[:, 2 * m + t, c * P:(c + 1) * P], ident)
                ins.then_inc(s["xt2_psum"], 1)
            pe.wait_ge(s["xt2_act"], 5)
            pe.wait_ge(s["xt2_dve"], 5)

            with pe.Fori(0, PAIRS) as q:
                for e in range(2):
                    pe.wait_ge(s[f"w_in{e}"], 32 * (q + 1))
                    for f in range(FC):
                        n = (2 * q + e) * FC + f
                        if f >= 4:
                            pe.wait_ge(s["h_act" if f % 2 == 0 else "h_dve"],
                                       (2 * q + e) * FC // 2 + (f - 4) // 2 + 1)
                        for c in range(KC):
                            ins = nc.tensor.matmul(ps[:, f % 4, 0:CAP], w1s[e][:, c, f * P:(f + 1) * P],
                                                   xt[:, c, bass.ds((2 * q + e) * CAP, CAP)],
                                                   start=(c == 0), stop=(c == KC - 1))
                        ins.then_inc(s["h_psum"], 1)
                    pe.wait_ge(s["o_done"], 2 * q + e)
                    for f in range(FC):
                        pe.wait_ge(s["h_act" if f % 2 == 0 else "h_dve"],
                                   (2 * q + e) * FC // 2 + f // 2 + 1)
                        for c in range(KC):
                            ins = nc.tensor.matmul(ps[:, 4 + c, 0:CAP], w2s[e][:, f, c * P:(c + 1) * P],
                                                   ht[e][:, f, :], start=(f == 0), stop=(f == FC - 1))
                    ins.then_inc(s["o_psum"], 1)
                pe.wait_ge(s["o_done"], 2 * q + 2)
                for t in range(PTILES):
                    if t == 0:
                        pe.wait_ge(s["t_act"], 3 * q)
                    elif t == 1:
                        pe.wait_ge(s["t_dve"], 2 * q)
                    elif t % 2 == 0:
                        pe.wait_ge(s["t_act"], 3 * q + t // 2)
                    else:
                        pe.wait_ge(s["t_dve"], 2 * q + t // 2)
                    for c in range(KC):
                        ins = nc.tensor.transpose(ps[:, 6 + t % 2, c * P:(c + 1) * P],
                                                  eot[:, c, t * P:(t + 1) * P], ident)
                    ins.then_inc(s["t_psum"], 1)

        @block.vector
        def _(dve):
            steps = [0]

            def link(ins):
                steps[0] += 1
                ins.then_inc(s["dve_step"], 1)
                dve.wait_ge(s["dve_step"], steps[0])

            dve.wait_ge(s["x_in"], 16)
            for j in range(TILES):
                ins = nc.vector.bn_stats(stats[:, j, :], xnat[:, j, :])
            link(ins)
            for j in range(TILES):
                ins = nc.vector.bn_aggr(mvz[:, j, :], stats[:, j, :])
            link(ins)
            nc.vector.tensor_scalar(rv[:], mvz[:, :, 1], EPS, None, ALU.add).then_inc(s["z_stats"], 1)
            dve.wait_ge(s["small_in"], 80)
            for hb in range(HALVES):
                for c in range(EC):
                    q = hb * EC + c
                    acc = conv[hb][:, c, :].rearrange("p (b l) -> p b l", b=HB)
                    src = ps[:, 2 + q, :].rearrange("p (b l) -> p b l", b=HB)
                    dve.wait_ge(s["conv_first"], q + 1)
                    for k in range(1, TAPS):
                        ins = nc.vector.scalar_tensor_tensor(
                            out=acc[:, :, k:L], in0=src[:, :, 0:L - k],
                            scalar=ch[:, c, CW + TAPS - 1 - k:CW + TAPS - k],
                            in1=acc[:, :, k:L], op0=ALU.mult, op1=ALU.add)
                        if k < TAPS - 1:
                            link(ins)
                    ins.then_inc(s["conv_done"], 1)
            dve.wait_ge(s["z_rstd"], 1)
            nc.vector.scalar_tensor_tensor(out=nmr[:], in0=mvz[:, :, 0], scalar=-1.0, in1=rstd[:],
                                           op0=ALU.mult, op1=ALU.mult).then_inc(s["z_scale"], 1)
            nc.vector.tensor_copy(tri[:], cst[:, CTRI:CTRI + P])
            for j in range(TILES):
                nc.vector.tensor_copy(xrow[:, j, :, DM + 1], cst[:, CDST + TOPK * j:CDST + TOPK * (j + 1)])
            for hb in range(HALVES):
                cols = slice(hb * HT, (hb + 1) * HT)
                dve.wait_ge(s["hi_done"], hb + 1)
                dve.wait_ge(s["stack_done"], hb)
                link(nc.vector.tensor_tensor(rest, ps[0:3 * BC, 6 + hb, :], stack[:, cols], ALU.subtract))
                nc.vector.tensor_copy(stack[BC:2 * BC, cols], rest[BC:2 * BC, :])
                link(nc.vector.tensor_copy(stack[2 * BC:3 * BC, cols], rest[2 * BC:3 * BC, :]))
                link(nc.vector.tensor_tensor(rest[2 * BC:3 * BC, :], rest[2 * BC:3 * BC, :],
                                             stack[2 * BC:3 * BC, cols], ALU.subtract))
                nc.vector.tensor_copy(stack[2 * BC:3 * BC, cols], rest[2 * BC:3 * BC, :]
                                      ).then_inc(s["stack_done"], 1)
            dve.wait_ge(s["act_step"], 1)
            nc.vector.tensor_scalar(anegs[:], anegs[:], -1.0, None, ALU.mult).then_inc(s["a_done"], 1)
            for c in range(EC):
                ins = nc.vector.tensor_scalar(diagd[:, c, :], ident, ch[:, c, DSK:DSK + 1], None, ALU.mult)
            ins.then_inc(s["a_done"], 1)
            for hb in range(HALVES):
                for c in range(EC):
                    q = hb * EC + c
                    d = delta[:, c, hb * HT:(hb + 1) * HT]
                    dve.wait_ge(s["sp_exp"], q + 1)
                    link(nc.vector.tensor_scalar(d, spe[hb][:, c, :], 1.0, -1.0, ALU.add, ALU.add))
                    link(nc.vector.tensor_tensor(d, spe[hb][:, c, :], d, ALU.subtract))
                    dve.wait_ge(s["sp_relu"], q + 1)
                    link(nc.vector.tensor_tensor(d, spr[hb][:, c, :], d, ALU.add))
                    dve.wait_ge(s["sp_ln"], q + 1)
                    nc.vector.tensor_tensor(d, spl[hb][:, c, :], d, ALU.add).then_inc(s["delta_done"], 1)
            for m in range(4):
                dve.wait_ge(s["zt_psum"], m + 1)
                nc.vector.tensor_copy(zst[:, 2 * m:2 * m + 2, :], ps[:, m % 2, :]
                                      .rearrange("p (j d) -> p j d", j=2)).then_inc(s["zt_done"], 1)
            for sl in range(2):
                nc.vector.memset(da[sl].rearrange("p c (b l) -> p (c b) l", l=L)[:, :, 0:1], 0.0
                                 ).then_inc(s["scan_done"], 1)

            dve.sem_inc(s["mult_done"], 2)

            def scan(g, par):
                dve.wait_ge(s["mult_done"], g + 1)
                dve.wait_ge(s["da_done"], EC * (g + 1))
                dve.wait_ge(s["dbu_done"], g + 3)
                nc.vector.tensor_tensor_scan(h[par].rearrange("p c t -> p (c t)"),
                                             da[par].rearrange("p c t -> p (c t)"),
                                             dbu[par].rearrange("p c t -> p (c t)"), 0.0,
                                             ALU.mult, ALU.add).then_inc(s["scan_done"], 1)

            def mult(g, par):
                dve.wait_ge(s["scan_done"], g + 3)
                dve.wait_ge(s["c_psum"], g + 1)
                dve.wait_ge(s["ysum_done"], g + 1)
                nc.vector.tensor_tensor(hc[par], h[par], cps[:, None, :].to_broadcast([P, EC, HT]),
                                        ALU.mult).then_inc(s["mult_done"], 1)

            for hb in range(HALVES):
                g0 = hb * DS
                scan(g0, 0)
                with dve.Fori(0, DS // 2 - 1) as i:
                    scan(g0 + 2 * i + 1, 1)
                    mult(g0 + 2 * i, 0)
                    scan(g0 + 2 * i + 2, 0)
                    mult(g0 + 2 * i + 1, 1)
                scan(g0 + DS - 1, 1)
                mult(g0 + DS - 2, 0)
                mult(g0 + DS - 1, 1)
                tiles = slice(hb * HTILES, (hb + 1) * HTILES)
                dve.wait_ge(s["ysum_done"], g0 + DS + 2)
                nc.vector.tensor_tensor(x1[:, tiles, :], y, zst[:, tiles, :], ALU.mult
                                        ).then_inc(s["x1_done"], 1)
                dve.wait_ge(s["x1_done"], 2 * hb + 1)
                nc.vector.tensor_tensor(x1[:, tiles, :], x1[:, tiles, :], xnat[:, tiles, :], ALU.add
                                        ).then_inc(s["x1_done"], 1)

            for hb in range(HALVES):
                tiles = slice(hb * HTILES, (hb + 1) * HTILES)
                j0 = hb * HTILES
                dve.wait_ge(s["x1_done"], 2 * hb + 2)
                for j in range(j0, j0 + HTILES):
                    ins = nc.vector.bn_stats(stats[:, j, :], x1[:, j, :])
                link(ins)
                for j in range(j0, j0 + HTILES):
                    ins = nc.vector.bn_aggr(mvx[:, j, :], stats[:, j, :])
                link(ins)
                nc.vector.tensor_scalar(rv[:, tiles], mvx[:, tiles, 1], EPS, None, ALU.add
                                        ).then_inc(s["ln_var"], 1)
                dve.wait_ge(s["ln_rstd"], hb + 1)
                for j in range(j0, j0 + HTILES):
                    ins = nc.vector.tensor_scalar(
                        xrow[:, j, :, 0:DM], x1[:, j:j + 1, :].to_broadcast([P, TOPK, DM]),
                        mvx[:, j, 0:1], rx[:, j:j + 1], ALU.subtract, ALU.mult)
                ins.then_inc(s["xn_done"], 1)
                dve.wait_ge(s["lg_psum"], hb + 1)
                logits = ps[:, 4, 0:HTILES * NE].rearrange("p (t e) -> p t e", e=NE)
                link(nc.vector.tensor_reduce(rmax[:, tiles], logits, AX.X, ALU.max))
                nc.vector.tensor_tensor(lg[:, tiles, :], logits,
                                        rmax[:, tiles, None].to_broadcast([P, HTILES, NE]), ALU.subtract
                                        ).then_inc(s["lg_sub"], 1)
                dve.wait_ge(s["lg_exp"], hb + 1)
                link(nc.vector.tensor_reduce(rsum[:, tiles], lg[:, tiles, :], AX.X, ALU.add))
                link(nc.vector.reciprocal(rsum[:, tiles], rsum[:, tiles]))
                link(nc.vector.tensor_tensor(lg[:, tiles, :], lg[:, tiles, :],
                                             rsum[:, tiles, None].to_broadcast([P, HTILES, NE]), ALU.mult))
                for j in range(j0, j0 + HTILES):
                    ins = nc.vector.max(top[:, j, :], lg[:, j, :])
                link(ins)
                for j in range(j0, j0 + HTILES):
                    ins = nc.vector.max_index(topi[:, j, :], top[:, j, :], lg[:, j, :])
                link(ins)
                nc.vector.tensor_copy(xrow[:, tiles, :, DM], top[:, tiles, 0:TOPK])
                link(nc.vector.tensor_copy(topf[:, tiles, :], topi[:, tiles, 0:TOPK]))
                link(nc.vector.tensor_tensor(
                    oh[:, tiles, :, :],
                    cst[:, None, None, CIOTA:CIOTA + NE].to_broadcast([P, HTILES, TOPK, NE]),
                    topf[:, tiles, :, None].to_broadcast([P, HTILES, TOPK, NE]), ALU.is_equal))
                nc.vector.tensor_tensor(multi[:, tiles, :], oh[:, tiles, 0, :], oh[:, tiles, 1, :], ALU.add
                                        ).then_inc(s["multi_done"], 1)
                dve.wait_ge(s["pos_psum"], hb + 1)
                cum = ps[:, 5, 0:HTILES * NE].rearrange("p (t e) -> p t e", e=NE)
                link(nc.vector.tensor_tensor(ohc[:, tiles, :, :], oh[:, tiles, :, :],
                                             cum[:, :, None, :].to_broadcast([P, HTILES, TOPK, NE]), ALU.mult))
                link(nc.vector.tensor_reduce(pos[:, tiles, :], ohc[:, tiles, :, :], AX.X, ALU.add))
                link(nc.vector.scalar_tensor_tensor(out=slot[:, tiles, :], in0=topf[:, tiles, :],
                                                    scalar=float(CAP), in1=pos[:, tiles, :],
                                                    op0=ALU.mult, op1=ALU.add))
                link(nc.vector.tensor_scalar(pos[:, tiles, :], pos[:, tiles, :], float(CAP), DROPPED,
                                             ALU.is_ge, ALU.mult))
                nc.vector.tensor_tensor(sloti[:, tiles, :], slot[:, tiles, :], pos[:, tiles, :], ALU.add
                                        ).then_inc(s["slots_done"], 1)

            for m in range(1, STILES // 2, 2):
                dve.wait_ge(s["xt2_psum"], m + 1)
                nc.vector.tensor_copy(
                    xt[:, :, 2 * m * P:(2 * m + 2) * P].rearrange("p c (t n) -> p c t n", n=P),
                    ps[:, m % 4, :].rearrange("p (t c n) -> p c t n", t=2, c=KC)).then_inc(s["xt2_dve"], 1)
            with dve.Fori(0, PAIRS) as q:
                dve.wait_ge(s["res_out"], 16 * PTILES * q)
                nc.vector.tensor_copy(dst[:, :, None], xe[:, bass.ds(q * PTILES, PTILES), DM + 1:ROW]
                                      ).then_inc(s["dst_done"], 1)
                for e in range(2):
                    for f in range(1, FC, 2):
                        dve.wait_ge(s["h_psum"], (2 * q + e) * FC + f + 1)
                        nc.vector.tensor_scalar(ht[e][:, f, :], ps[:, f % 4, 0:CAP], 0.0, None, ALU.max
                                                ).then_inc(s["h_dve"], 1)
                for t in range(1, PTILES, 2):
                    dve.wait_ge(s["t_psum"], q * PTILES + t + 1)
                    nc.vector.tensor_scalar(eo[:, t, :], ps[:, 6 + t % 2, 0:DM],
                                            xe[:, bass.ds(q * PTILES + t, 1), DM:DM + 1]
                                            .rearrange("p a b -> p (a b)"), None, ALU.mult
                                            ).then_inc(s["t_dve"], 1)
            for q in range(4):
                tiles = slice(2 * q, 2 * q + 2)
                dve.wait_ge(s[f"res_in{q}"], 32)
                link(nc.vector.tensor_tensor(x1[:, tiles, :], x1[:, tiles, :], resl[:, 0, tiles, :], ALU.add))
                nc.vector.tensor_tensor(x1[:, tiles, :], x1[:, tiles, :], resl[:, 1, tiles, :], ALU.add
                                        ).then_inc(s["sum_done"], 1)


def kernel(x, ctx_1024, L0_xattn_in_proj_w, L0_xattn_conv_w, L0_xattn_conv_b, L0_xattn_x_proj_w,
           L0_xattn_dt_proj_w, L0_xattn_dt_proj_b, L0_xattn_A_log, L0_xattn_D, L0_ffn_Wg, L0_ffn_w1,
           L0_ffn_w2):
    import ml_dtypes
    from concourse import bacc
    from concourse.bass_utils import run_bass_kernel_spmd

    def by_chunk(a):
        a = np.asarray(a)
        return a.reshape(a.shape[0] // P, P, -1).transpose(1, 0, 2)

    x_proj = np.asarray(L0_xattn_x_proj_w).T
    chan = np.concatenate([np.asarray(L0_xattn_conv_w)] + [np.asarray(a).reshape(DI, -1) for a in (
        L0_xattn_conv_b, L0_xattn_dt_proj_b, L0_xattn_D, L0_xattn_A_log)], axis=1)
    consts = np.zeros((P, NCONST), np.float32)
    consts[:, CID:CID + P] = np.eye(P)
    consts[:, CTRI:CTRI + P] = np.triu(np.ones((P, P)), 1)
    for j in range(TILES):
        for k in range(TOPK):
            consts[:, CDST + TOPK * j + k] = k * T + j * P + np.arange(P)
    consts[:, CIOTA:CIOTA + NE] = np.arange(NE)
    sel = np.zeros((3, BC, BC, P), ml_dtypes.bfloat16)
    for n in range(BC):
        sel[:, n, n, :] = 1.0

    arrays = {
        "x": by_chunk(np.asarray(x).reshape(T, DM)),
        "ctx_t": np.asarray(ctx_1024).reshape(T, DC).T,
        "inproj_t": np.asarray(L0_xattn_in_proj_w).T,
        "xproj_t": by_chunk(np.concatenate([x_proj[:, 0:DR]] + [x_proj[:, DR:]] * 3, axis=1)),
        "dtproj_t": np.asarray(L0_xattn_dt_proj_w).T,
        "chan": by_chunk(chan),
        "wg": by_chunk(L0_ffn_Wg),
        "w1": np.asarray(L0_ffn_w1).reshape(NE, KC, P, DFF).transpose(0, 2, 1, 3),
        "w2": np.asarray(L0_ffn_w2).reshape(NE, FC, P, DM).transpose(0, 2, 1, 3),
        "consts": consts,
        "sel": sel.reshape(3 * BC, BC * P),
    }
    nc = bacc.Bacc("TRN2", target_bir_lowering=False, num_devices=1)
    ins, feed = {}, {}
    for name, a in arrays.items():
        a = np.ascontiguousarray(a)
        feed["in_" + name] = a
        ins[name] = nc.dram_tensor("in_" + name, a.shape, mybir.dt.from_np(a.dtype), kind="ExternalInput").ap()
    out = nc.dram_tensor("out", [T, DM], F32, kind="ExternalOutput").ap()
    build(nc, out=out, **ins)
    r = run_bass_kernel_spmd(nc, [feed], core_ids=[0])
    return r.results[0]["out"].reshape(B, L, DM)
```

```python
from contextlib import ExitStack

import numpy as np

import concourse.bass as bass
from concourse import mybir

F32 = mybir.dt.float32
F32R = mybir.dt.float32r
BF16 = mybir.dt.bfloat16
U32 = mybir.dt.uint32
ALU = mybir.AluOpType
ACT = mybir.ActivationFunctionType
AX = mybir.AxisListType

P = 128
B, L, DM = 4, 256, 256
DC = 128
DI, DS, TAPS, DR = 256, 16, 4, 8
EC = DI // P
T = B * L
TILES = T // P
HALVES = 2
HT = T // HALVES
HTILES = HT // P
HB = B // HALVES
NE, TOPK, DFF = 8, 2, 1024
CAP = (5 * T * TOPK // NE + 3) // 4
SLOTS = NE * CAP
ET = (CAP + P - 1) // P
EROWS = [min(P, CAP - t * P) for t in range(ET)]
FC = DFF // P
KC = DM // P
ROW = DM + 2
NROWS = T * TOPK
DROPPED = 8192.0
EPS = 1e-5
CB, DTB, DSK, ALOG, NCH = 0, 1, 2, 3, 3 + DS
CID, CTRI, CDST = 0, P, 2 * P
CIOTA = CDST + TILES * TOPK
NCONST = CIOTA + NE
BC = 2 * DS
XPC = 3 * BC + DR
WP = 4
FP = FC // WP
PROJ, DELTA, TURN, LOGIT, COUNT = 2, 3, 2, 4, 10
LEAD = 3


def halves(hb):
    return slice(hb * HT, (hb + 1) * HT)


def build(nc, x, ctx_t, inproj_t, xproj_t, dtproj_t, conv_w, chan, wg, w1, w2, consts, sel, out):
    xe_dram = nc.dram_tensor("expert_rows", [SLOTS, ROW], F32, kind="Internal").ap()
    res_dram = nc.dram_tensor("result_rows", [NROWS, DM], F32, kind="Internal").ap()

    with ExitStack() as ctx:
        def alloc(stack, name, shape, dt=F32):
            return stack.enter_context(nc.sbuf_tensor(name, shape, dt))

        def sb(name, shape, dt=F32):
            return alloc(ctx, name, shape, dt)

        cst = sb("cst", [P, NCONST])
        ident = cst[:, CID:CID + P]
        ch = sb("ch", [P, EC, NCH])
        x1 = sb("x1", [P, TILES, DM])
        wgs = sb("wgs", [P, KC, NE])
        w1raw = sb("w1raw", [P, KC, DFF])
        w2raw = sb("w2raw", [P, FC, DM])
        w1hi = sb("w1hi", [P, KC, DFF], F32R)
        w1lo = sb("w1lo", [P, KC, DFF], F32R)
        anegs = sb("anegs", [P, EC, DS])
        diagd = sb("diagd", [P, EC, P])
        tri = sb("tri", [P, P], BF16)
        ones = sb("ones", [P, P], BF16)
        onesf = sb("onesf", [P, P])
        fill = sb("fill", [P, ROW])
        nhalf = sb("nhalf", [P, TILES])
        stats = sb("stats", [P, TILES, 6])
        mvz = sb("mvz", [P, TILES, 2])
        mvx = sb("mvx", [P, TILES, 2])
        vz = sb("vz", [P, TILES])
        rz = sb("rz", [P, TILES])
        nmz = sb("nmz", [P, TILES])
        vx = sb("vx", [P, TILES])
        rx = sb("rx", [P, TILES])
        nmx = sb("nmx", [P, TILES])
        lg = sb("lg", [P, TILES, NE])
        top = sb("top", [P, TILES, NE])
        etop = sb("etop", [P, TILES, NE])
        topi = sb("topi", [P, TILES, NE], U32)
        topf = sb("topf", [P, TILES, TOPK])
        rsum = sb("rsum", [P, TILES])
        oh = sb("oh", [P, TILES, TOPK, NE])
        ohc = sb("ohc", [P, TILES, TOPK, NE])
        cum = sb("cum", [P, HTILES, NE])
        multi = sb("multi", [P, TILES, NE], BF16)
        pos = sb("pos", [P, TILES, TOPK])
        slot = sb("slot", [P, TILES, TOPK])
        sloti = sb("sloti", [P, TILES, TOPK], U32)
        gates = sb("gates", [P, NE * ET, 1])
        dst = sb("dst", [P, NE * ET, 1], U32)

        scan_mem = ExitStack()

        def sm(name, shape, dt=F32):
            return alloc(scan_mem, name, shape, dt)

        xnat = sm("xnat", [P, TILES, DM])
        zst = sm("zst", [P, TILES, DM])
        xrow = sm("xrow", [P, TILES, TOPK, ROW])
        inps = sm("inps", [P, DI])
        cwb = sm("cwb", [P, TAPS, DI])
        ctxs = sm("ctxs", [P, T])
        xps = sm("xps", [P, EC, XPC])
        dtps = sm("dtps", [3 * BC + DR, DI])
        dtlo = sm("dtlo", [3 * BC + DR, T])
        u = sm("u", [P, EC, T])
        delta = sm("delta", [P, EC, T])
        du = sm("du", [P, EC, T])
        sels = sm("sels", [3 * BC, BC * P], BF16)
        stack = sm("stack", [3 * BC, T], BF16)
        rest = sm("rest", [3 * BC, HT])
        zs = sm("zs", [P, TILES, DM])
        spr = [sm(f"spr{i}", [P, EC, HT]) for i in range(HALVES)]
        spe1 = sm("spe1", [P, EC, HT])
        spl1 = sm("spl1", [P, EC, HT])
        bsb = [sm(f"bsb{i}", [P, HT]) for i in range(2)]
        dbu = [sm(f"dbu{i}", [P, EC, HT]) for i in range(2)]
        h = [sm(f"h{i}", [P, EC, HT]) for i in range(2)]
        hc = [sm(f"hc{i}", [P, EC, HT]) for i in range(2)]
        spe, spl = [hc[0], spe1], [dbu[0], spl1]
        xnt = spr[0]
        scan_mem.close()

        w2hi = sb("w2hi", [P, FC, DM], F32R)
        w2lo = sb("w2lo", [P, FC, DM], F32R)
        xe = sb("xe", [P, ET, ROW])
        xthi = sb("xthi", [P, KC, SLOTS], F32R)
        xtlo = sb("xtlo", [P, KC, SLOTS], F32R)
        hthi = sb("hthi", [P, FC, CAP], F32R)
        htlo = sb("htlo", [P, FC, CAP], F32R)
        eot = sb("eot", [P, KC, CAP])
        eo = sb("eo", [P, ET, DM])
        resl = sb("resl", [P, TOPK, TILES, DM])

        ps = ctx.enter_context(nc.psum_tensor("ps", [P, 8, HT], F32))
        y = ps[:, 0:2, :].rearrange("p b (t e) -> p (b t) e", e=DI)
        da = [ps[:, 2:4, :], ps[:, 4:6, :]]
        CBANK, BBANK = 6, 7
        PBANK, DBANK, LBANK = [CBANK, BBANK], [2, 3, BBANK, BBANK], [[BBANK, BBANK], [4, 5]]

        s = {n: ctx.enter_context(nc.semaphore(n)) for n in (
            "ctx_in0 ctx_in1 inp_in x_in small_in sel_in w1_in w2_in xe_in fill_made xe_filled res_filled "
            "z_stats z_rstd z_scale zs_done zt_psum zt_done wg_psum wg_done "
            "cw_in ch_in cw_done conv_psum u_done xp_psum dtlo_done hi_done stack_done "
            "dt_psum sp_abs sp_exp sp_relu sp_sum sp_ln delta_done du_done a_exp a_done "
            "b_psum b_done c_psum da_done scan_done dbu_done mult_done ysum_done "
            "y_used x1_done ln_var ln_rstd ln_scale xn_done xt_psum xt_done lg_psum lg_done top_sub top_exp "
            "multi_done pos_psum pos_done gates_done slots_done scattered "
            "w1hi_done w1lo_done w2hi_done w2lo_done xet_psum xthi_done xtlo_done meta_done "
            "h_psum hthi_done htlo_done o_psum o_done r_psum r_act r_dve res_out "
            "res_in0 res_in1 res_in2 res_in3 sum_done out_done dve_step").split()}

        block = ctx.enter_context(nc.Block())

        @block.sync
        def _(sp):
            sp.dma_start(inps[:], inproj_t).then_inc(s["inp_in"], 16)
            for hb in range(HALVES):
                sp.dma_start(ctxs[:, halves(hb)], ctx_t[:, halves(hb)]).then_inc(s[f"ctx_in{hb}"], 16)
            sp.dma_start(xnat[:], x).then_inc(s["x_in"], 16)
            sp.dma_start(cst[:], consts).then_inc(s["small_in"], 16)
            sp.dma_start(dtps[3 * BC:3 * BC + DR, :], dtproj_t).then_inc(s["small_in"], 16)
            sp.dma_start(wgs[:], wg).then_inc(s["small_in"], 16)
            sp.dma_start(sels[:], sel).then_inc(s["sel_in"], 16)
            sp.dma_start(w1raw[:], w1[0]).then_inc(s["w1_in"], 16)
            sp.dma_start(w2raw[:], w2[0]).then_inc(s["w2_in"], 16)
            sp.wait_ge(s["fill_made"], 1)
            sp.dma_start(xe_dram.rearrange("(t p) r -> p t r", p=P),
                         fill[:, None, :].to_broadcast([P, SLOTS // P, ROW])).then_inc(s["xe_filled"], 16)
            sp.dma_start(res_dram.rearrange("(t p) r -> p t r", p=P),
                         fill[:, None, 0:DM].to_broadcast([P, NROWS // P, DM])).then_inc(s["res_filled"], 16)

            def rows_in(e):
                sp.dma_start(xe[:, 0:2, :], xe_dram[e * CAP:e * CAP + 2 * P].rearrange("(t p) r -> p t r", p=P)).then_inc(s["xe_in"], 16)
                sp.dma_start(xe[0:EROWS[2], 2, :], xe_dram[e * CAP + 2 * P:(e + 1) * CAP]).then_inc(s["xe_in"], 16)

            sp.wait_ge(s["scattered"], 16 * TILES * TOPK)
            rows_in(0)
            for e in range(1, NE):
                sp.wait_ge(s["w1hi_done"], WP * e)
                sp.wait_ge(s["w1lo_done"], WP * e)
                sp.dma_start(w1raw[:], w1[e]).then_inc(s["w1_in"], 16)
                sp.wait_ge(s["xet_psum"], e)
                sp.wait_ge(s["meta_done"], 2 * e)
                rows_in(e)
                sp.wait_ge(s["w2hi_done"], WP * e)
                sp.wait_ge(s["w2lo_done"], WP * e)
                sp.dma_start(w2raw[:], w2[e]).then_inc(s["w2_in"], 16)
            sp.wait_ge(s["res_out"], 16 * NE * ET)
            for q in range(4):
                for k in range(TOPK):
                    rows = res_dram[k * T + q * 2 * P:k * T + (q + 1) * 2 * P]
                    sp.dma_start(resl[:, k, 2 * q:2 * q + 2, :],
                                 rows.rearrange("(t p) d -> p t d", p=P)).then_inc(s[f"res_in{q}"], 16)
            for q in range(4):
                sp.wait_ge(s["sum_done"], q + 1)
                sp.dma_start(out[q * 2 * P:(q + 1) * 2 * P].rearrange("(t p) d -> p t d", p=P),
                             x1[:, 2 * q:2 * q + 2, :]).then_inc(s["out_done"], 16)
            sp.wait_ge(s["out_done"], 64)

        @block.gpsimd
        def _(pool):
            nc.gpsimd.memset(onesf[:], 1.0)
            nc.gpsimd.memset(ones[:], 1.0)
            nc.gpsimd.memset(nhalf[:], -0.5)
            nc.gpsimd.memset(fill[:, 0:DM + 1], 0.0)
            nc.gpsimd.memset(fill[:, DM + 1:ROW], DROPPED).then_inc(s["fill_made"], 1)
            pool.sem_inc(s["dbu_done"], 2)
            pool.wait_ge(s["z_stats"], 1)
            pool.wait_ge(s["fill_made"], 1)
            nc.gpsimd.tensor_tensor(rz[:], vz[:], nhalf[:], ALU.pow).then_inc(s["z_rstd"], 1)
            def max_plus_exp(hb):
                for c in range(EC):
                    pool.wait_ge(s["sp_relu"], hb * EC + c + 1)
                    pool.wait_ge(s["sp_exp"], hb * EC + c + 1)
                    nc.gpsimd.tensor_tensor(spr[hb][:, c, :], spr[hb][:, c, :], spe[hb][:, c, :], ALU.add
                                            ).then_inc(s["sp_sum"], 1)

            def delta_u(hb):
                for c in range(EC):
                    pool.wait_ge(s["delta_done"], EC * hb + c + 1)
                    nc.gpsimd.tensor_tensor(du[:, c, halves(hb)], delta[:, c, halves(hb)],
                                            u[:, c, halves(hb)], ALU.mult).then_inc(s["du_done"], 1)

            def step(hb, g, par):
                pool.wait_ge(s["b_done"], g + 1)
                pool.wait_ge(s["scan_done"], g + 1)
                nc.gpsimd.tensor_tensor(dbu[par][:], du[:, :, halves(hb)],
                                        bsb[par][:, None, :].to_broadcast([P, EC, HT]), ALU.mult
                                        ).then_inc(s["dbu_done"], 1)

            def row_rstd(hb):
                tiles = slice(hb * HTILES, (hb + 1) * HTILES)
                pool.wait_ge(s["ln_var"], hb + 1)
                nc.gpsimd.tensor_tensor(rx[:, tiles], vx[:, tiles], nhalf[:, tiles], ALU.pow
                                        ).then_inc(s["ln_rstd"], 1)

            def send(hb):
                pool.wait_ge(s["gates_done"], hb + 1)
                pool.wait_ge(s["slots_done"], hb + 1)
                for j in range(hb * HTILES, (hb + 1) * HTILES):
                    pool.wait_ge(s["xn_done"], j + 1)
                    for k in range(TOPK):
                        nc.gpsimd.indirect_dma_start(
                            xe_dram, bass.IndirectOffsetOnAxis(ap=sloti[:, j, k:k + 1], axis=0),
                            xrow[:, j, k, :], None, bounds_check=SLOTS - 1, oob_is_err=False
                        ).then_inc(s["scattered"], 16)

            max_plus_exp(0)
            delta_u(0)
            pool.wait_ge(s["du_done"], EC)
            step(0, 0, 0)
            step(0, 1, 1)
            def steps(hb, lo, hi):
                with pool.Fori(lo, hi) as i:
                    for par in range(2):
                        step(hb, hb * DS + 2 * i + par, par)

            steps(0, 1, 4)
            max_plus_exp(1)
            steps(0, 4, 6)
            delta_u(1)
            steps(0, 6, DS // 2)
            pool.wait_ge(s["du_done"], EC * HALVES)
            for n in range(4):
                step(1, DS + n, n % 2)
            row_rstd(0)
            steps(1, 2, DS // 2)
            pool.wait_ge(s["xe_filled"], 16)
            send(0)
            row_rstd(1)
            send(1)
            pool.wait_ge(s["res_filled"], 16)

            def send_results(e):
                for t in range(ET):
                    if t < 2:
                        pool.wait_ge(s["r_act"], 2 * e + t + 1)
                    else:
                        pool.wait_ge(s["r_dve"], e + 1)
                    nc.gpsimd.indirect_dma_start(
                        res_dram, bass.IndirectOffsetOnAxis(ap=dst[0:EROWS[t], e * ET + t, :], axis=0),
                        eo[0:EROWS[t], t, :], None, bounds_check=NROWS - 1, oob_is_err=False
                    ).then_inc(s["res_out"], 16)

            for e in range(NE):
                pool.wait_ge(s["w2_in"], 16 * (e + 1))
                for m in range(WP):
                    fs = slice(m * FP, (m + 1) * FP)
                    pool.wait_ge(s["w2hi_done"], WP * e + m + 1)
                    nc.gpsimd.tensor_tensor(w2lo[:, fs, :], w2raw[:, fs, :], w2hi[:, fs, :].bitcast(F32),
                                            ALU.subtract).then_inc(s["w2lo_done"], 1)
                if e >= 1:
                    send_results(e - 1)
            send_results(NE - 1)

        @block.scalar
        def _(act):
            act.dma_start(cwb[:], conv_w[None, :, :].to_broadcast([P, TAPS, DI])).then_inc(s["cw_in"], 16)
            act.dma_start(ch[:], chan).then_inc(s["ch_in"], 16)
            act.dma_start(xps[:], xproj_t).then_inc(s["small_in"], 16)

            def conv_silu(hb):
                for c in range(EC):
                    act.wait_ge(s["conv_psum"], hb * EC + c + 1)
                    nc.scalar.activation(u[:, c, halves(hb)], ps[:, 2 + hb * EC + c, :], ACT.Silu,
                                         bias=ch[:, c, CB:CB + 1]).then_inc(s["u_done"], 1)

            def parts(hb):
                act.wait_ge(s["xp_psum"], hb + 1)
                nc.scalar.activation(dtlo[3 * BC:3 * BC + DR, halves(hb)],
                                     ps[3 * BC:3 * BC + DR, PBANK[hb], :], ACT.Copy
                                     ).then_inc(s["dtlo_done"], 1)
                if hb:
                    act.wait_ge(s["stack_done"], hb)
                nc.scalar.activation(rest[:], ps[0:3 * BC, PBANK[hb], :], ACT.Copy)
                nc.scalar.activation(stack[:, halves(hb)], ps[0:3 * BC, PBANK[hb], :], ACT.Copy
                                     ).then_inc(s["hi_done"], 1)

            def z_silu(tiles):
                for j in tiles:
                    ins = nc.scalar.activation(zs[:, j, :], xnat[:, j, :], ACT.Silu,
                                               bias=nmz[:, j:j + 1], scale=rz[:, j:j + 1])
                ins.then_inc(s["zs_done"], 1)

            def exps(hb, c):
                q = hb * EC + c
                v = ps[:, DBANK[q], :]
                act.wait_ge(s["dt_psum"], q + 1)
                nc.scalar.activation(spe[hb][:, c, :], v, ACT.Abs, bias=ch[:, c, DTB:DTB + 1]
                                     ).then_inc(s["sp_abs"], 1)
                nc.scalar.activation(spr[hb][:, c, :], v, ACT.Relu, bias=ch[:, c, DTB:DTB + 1]
                                     ).then_inc(s["sp_relu"], 1)
                act.wait_ge(s["sp_abs"], q + 1)
                nc.scalar.activation(spe[hb][:, c, :], spe[hb][:, c, :], ACT.Exp, scale=-1.0
                                     ).then_inc(s["sp_exp"], 1)

            def logs(hb):
                for c in range(EC):
                    act.wait_ge(s["sp_exp"], hb * EC + c + 1)
                    nc.scalar.activation(spl[hb][:, c, :], spe[hb][:, c, :], ACT.Ln, bias=1.0
                                         ).then_inc(s["sp_ln"], 1)

            act.wait_ge(s["ch_in"], 16)
            conv_silu(0)
            act.wait_ge(s["z_scale"], 1)
            z_silu(range(0, 4))
            parts(0)
            z_silu(range(4, 8))
            nc.scalar.activation(anegs[:], ch[:, :, ALOG:ALOG + DS], ACT.Exp).then_inc(s["a_exp"], 1)
            for c in range(EC):
                exps(0, c)
            logs(0)
            conv_silu(1)

            def b_copy(g, par):
                act.wait_ge(s["b_psum"], g + 1)
                act.wait_ge(s["dbu_done"], g + 1)
                nc.scalar.activation(bsb[par][:], ps[:, BBANK, :], ACT.Copy).then_inc(s["b_done"], 1)

            def decay(g, par):
                hb, n = g // DS, g % DS
                act.wait_ge(s["scan_done"], g + 1)
                for c in range(EC):
                    if g == 0:
                        act.wait_ge(s["delta_done"], c + 1)
                    nc.scalar.activation(
                        da[par][:, c, :].rearrange("p (b l) -> p b l", b=HB)[:, :, 1:L],
                        delta[:, c, halves(hb)].rearrange("p (b l) -> p b l", b=HB)[:, :, 1:L],
                        ACT.Exp, scale=anegs[:, c, n:n + 1]).then_inc(s["da_done"], 1)

            def x1_turned(hb, m):
                act.wait_ge(s["xt_psum"], 2 * hb + m + 1)
                nc.scalar.activation(xnt[:, :, m * 2 * P:(m + 1) * 2 * P],
                                     ps[:, BBANK - hb * (1 - m), :].rearrange("p (c t) -> p c t", c=KC),
                                     ACT.Copy).then_inc(s["xt_done"], 1)

            def logits_out(hb, m):
                act.wait_ge(s["lg_psum"], 2 * hb + m + 1)
                nc.scalar.activation(lg[:, hb * HTILES + 2 * m:hb * HTILES + 2 * m + 2, :],
                                     ps[:, LBANK[hb][m], 0:2 * NE].rearrange("p (t e) -> p t e", e=NE),
                                     ACT.Copy).then_inc(s["lg_done"], 1)

            def counts_out(hb):
                act.wait_ge(s["pos_psum"], hb + 1)
                nc.scalar.activation(cum[:], ps[:, LBANK[hb][0], 0:HTILES * NE].rearrange("p (t e) -> p t e", e=NE),
                                     ACT.Copy).then_inc(s["pos_done"], 1)

            def normalise(j):
                act.wait_ge(s["ln_scale"], j // HTILES + 1)
                nc.scalar.activation(xrow[:, j, :, 0:DM],
                                     x1[:, j:j + 1, :].to_broadcast([P, TOPK, DM]), ACT.Identity,
                                     bias=nmx[:, j:j + 1], scale=rx[:, j:j + 1]).then_inc(s["xn_done"], 1)

            def top_exp(hb):
                act.wait_ge(s["top_sub"], hb + 1)
                tiles = slice(hb * HTILES, (hb + 1) * HTILES)
                nc.scalar.activation(etop[:, tiles, :], etop[:, tiles, :], ACT.Exp).then_inc(s["top_exp"], 1)

            act.wait_ge(s["a_done"], 2)
            for g in range(HALVES * DS):
                if g == 0:
                    b_copy(0, 0)
                if g == DS:
                    act.wait_ge(s["delta_done"], EC * HALVES)
                decay(g, g % 2)
                n = g - LEAD
                if n == PROJ:
                    parts(1)
                if n in (DELTA, DELTA + 1):
                    exps(1, n - DELTA)
                if n == DELTA + 1:
                    logs(1)
                n -= DS
                if n in (TURN, TURN + 1):
                    x1_turned(0, n - TURN)
                if n in (LOGIT, LOGIT + 1):
                    logits_out(0, n - LOGIT)
                if n == COUNT:
                    counts_out(0)
                if g + 1 < HALVES * DS:
                    b_copy(g + 1, 1 - g % 2)
                if LOGIT + 2 <= n < LOGIT + 2 + HTILES:
                    normalise(n - LOGIT - 2)
                if n == COUNT:
                    top_exp(0)
            x1_turned(1, 0)
            x1_turned(1, 1)
            normalise(HTILES)
            normalise(HTILES + 1)
            logits_out(1, 0)
            logits_out(1, 1)
            top_exp(1)
            counts_out(1)
            normalise(HTILES + 2)
            normalise(HTILES + 3)

            def split_w1(e, m):
                cols = slice(m * FP * P, (m + 1) * FP * P)
                act.wait_ge(s["w1_in"], 16 * (e + 1))
                act.wait_ge(s["h_psum"], FC * e)
                nc.scalar.activation(w1hi[:, :, cols], w1raw[:, :, cols], ACT.Copy
                                     ).then_inc(s["w1hi_done"], 1)

            def split_w2(e, m):
                fs = slice(m * FP, (m + 1) * FP)
                act.wait_ge(s["w2_in"], 16 * (e + 1))
                act.wait_ge(s["o_psum"], e)
                nc.scalar.activation(w2hi[:, fs, :], w2raw[:, fs, :], ACT.Copy).then_inc(s["w2hi_done"], 1)

            def rows_hi(e):
                act.wait_ge(s["xet_psum"], e + 1)
                nc.scalar.activation(xthi[:, :, bass.ds(e * CAP, CAP)], ps[:, 6:8, 0:CAP], ACT.Copy
                                     ).then_inc(s["xthi_done"], 1)

            def hidden_hi(e, f):
                act.wait_ge(s["h_psum"], e * FC + f + 1)
                nc.scalar.activation(hthi[:, f, :], ps[:, f % 4, 0:CAP], ACT.Relu).then_inc(s["hthi_done"], 1)

            def gated_rows(e):
                act.wait_ge(s["r_psum"], e + 1)
                act.wait_ge(s["res_out"], 16 * ET * e)
                for t in range(2):
                    nc.scalar.activation(eo[:, t, :], ps[:, 6, t * DM:(t + 1) * DM], ACT.Copy,
                                         scale=gates[:, bass.ds(e * ET + t, 1), 0]).then_inc(s["r_act"], 1)

            def expert(e, first, last):
                for f in range(FC):
                    hidden_hi(e, f)
                    if f < WP:
                        split_w2(e, f)
                    if f == FC // 2 + 1 and not first:
                        gated_rows(e - 1)
                if not last:
                    rows_hi(e + 1)
                    for m in range(WP):
                        split_w1(e + 1, m)
                act.wait_ge(s["o_psum"], e + 1)
                nc.scalar.activation(eot[:], ps[:, 4:6, 0:CAP], ACT.Copy).then_inc(s["o_done"], 1)

            for m in range(WP):
                split_w1(0, m)
            rows_hi(0)
            expert(0, True, False)
            with act.Fori(1, NE - 1) as e:
                expert(e, False, False)
            expert(NE - 1, False, True)
            gated_rows(NE - 1)

        @block.tensor
        def _(pe):
            pe.sem_inc(s["ysum_done"], 2)
            def conv(hb):
                for c in range(EC):
                    acc = ps[:, 2 + hb * EC + c, :].rearrange("p (b l) -> p b l", b=HB)
                    src = ctxs[:, halves(hb)].rearrange("p (b l) -> p b l", b=HB)
                    for k in range(TAPS):
                        ins = nc.tensor.matmul(acc[:, :, k:L], cwb[:, TAPS - 1 - k, c * P:(c + 1) * P],
                                               src[:, :, 0:L - k], start=(k == 0), stop=(k == TAPS - 1),
                                               skip_group_check=True)
                    ins.then_inc(s["conv_psum"], 1)

            def x_proj(hb):
                pe.wait_ge(s["u_done"], EC * (hb + 1))
                for c in range(EC):
                    ins = nc.tensor.matmul(ps[0:XPC, PBANK[hb], :], xps[:, c, :], u[:, c, halves(hb)],
                                           start=(c == 0), stop=(c == EC - 1))
                ins.then_inc(s["xp_psum"], 1)

            def dt_proj(hb, c):
                pe.wait_ge(s["dtlo_done"], hb + 1)
                nc.tensor.matmul(ps[:, DBANK[hb * EC + c], :], dtps[3 * BC:3 * BC + DR, c * P:(c + 1) * P],
                                 dtlo[3 * BC:3 * BC + DR, halves(hb)], start=True, stop=True
                                 ).then_inc(s["dt_psum"], 1)

            def z_turn(m):
                for n in range(4):
                    j, c = 2 * m + n // 2, n % 2
                    ins = nc.tensor.transpose(
                        ps[:, m % 2, n * P:(n + 1) * P],
                        zs[:, (j // 2) * 2 + c, (j % 2) * P:(j % 2 + 1) * P], ident)
                ins.then_inc(s["zt_psum"], 1)

            def b_cast(hb, g, n):
                pe.wait_ge(s["b_done"], g)
                nc.tensor.matmul(ps[:, BBANK, :], sels[:, bass.ds(n * P, P)], stack[:, halves(hb)],
                                 start=True, stop=True).then_inc(s["b_psum"], 1)

            def c_cast(hb, g, n):
                pe.wait_ge(s["mult_done"], g + 2)
                nc.tensor.matmul(ps[:, CBANK, :], sels[:, bass.ds((DS + n) * P, P)], stack[:, halves(hb)],
                                 start=True, stop=True).then_inc(s["c_psum"], 1)

            def state_sum(g, par, last=False):
                pe.wait_ge(s["mult_done"], g + 3)
                for t in range(HTILES):
                    for c in range(EC):
                        ins = nc.tensor.matmul(y[:, t, c * P:(c + 1) * P], hc[par][:, c, t * P:(t + 1) * P],
                                               ident, start=False, stop=last, skip_group_check=True)
                ins.then_inc(s["ysum_done"], 1)

            def turn_x1(hb, m):
                pe.wait_ge(s["x1_done"], 2 * hb + m + 1)
                for c in range(KC):
                    for t in range(2):
                        ins = nc.tensor.transpose(
                            ps[:, BBANK - hb * (1 - m), (2 * c + t) * P:(2 * c + t + 1) * P],
                            x1[:, hb * HTILES + 2 * m + t, c * P:(c + 1) * P], ident)
                ins.then_inc(s["xt_psum"], 1)

            def logits(hb, m):
                pe.wait_ge(s["wg_done"], 1)
                pe.wait_ge(s["xt_done"], 2 * hb + m + 1)
                for t in range(2):
                    for c in range(KC):
                        tile = 2 * m + t
                        ins = nc.tensor.matmul(ps[:, LBANK[hb][m], t * NE:(t + 1) * NE],
                                               xnt[:, c, tile * P:(tile + 1) * P], wgs[:, c, :],
                                               start=(t == 0 and c == 0), stop=(c == KC - 1),
                                               skip_group_check=True)
                ins.then_inc(s["lg_psum"], 1)

            def counts(hb):
                pe.wait_ge(s["multi_done"], hb + 1)
                before = ps[:, LBANK[hb][0], 0:HTILES * NE].rearrange("p (t e) -> p t e", e=NE)
                mh = multi[:, hb * HTILES:(hb + 1) * HTILES, :]
                last = nc.tensor.matmul(before, tri[:], mh, start=True, stop=False, skip_group_check=True)
                for t in range(1, HTILES):
                    last = nc.tensor.matmul(before[:, t:HTILES, :], ones[:], mh[:, 0:HTILES - t, :],
                                            start=False, stop=False, skip_group_check=True)
                for j in range(hb * HTILES):
                    last = nc.tensor.matmul(before, ones[:], multi[:, j:j + 1, :].to_broadcast([P, HTILES, NE]),
                                            start=False, stop=False, skip_group_check=True)
                last.then_inc(s["pos_psum"], 1)

            pe.wait_ge(s["ctx_in0"], 16)
            pe.wait_ge(s["cw_done"], 1)
            conv(0)
            pe.wait_ge(s["small_in"], 64)
            pe.wait_ge(s["fill_made"], 1)
            for c in range(KC):
                ins = nc.tensor.matmul(ps[:, 0, 0:NE], onesf[:], wgs[:, c, :], start=(c == 0),
                                       stop=(c == KC - 1))
            ins.then_inc(s["wg_psum"], 1)
            x_proj(0)
            for c in range(EC):
                dt_proj(0, c)
            pe.wait_ge(s["ctx_in1"], 16)
            conv(1)
            pe.wait_ge(s["sel_in"], 16)
            pe.wait_ge(s["stack_done"], 1)
            b_cast(0, 0, 0)
            pe.wait_ge(s["wg_done"], 1)
            for m in range(4):
                pe.wait_ge(s["zs_done"], m // 2 + 1)
                if m >= 2:
                    pe.wait_ge(s["zt_done"], m - 1)
                z_turn(m)
            b_cast(0, 1, 1)

            def open_sums(hb):
                for t in range(HTILES):
                    for c in range(EC):
                        nc.tensor.matmul(y[:, t, c * P:(c + 1) * P],
                                         u[:, c, hb * HT + t * P:hb * HT + (t + 1) * P], diagd[:, c, :],
                                         start=(t % 2 == 0 and c == 0), stop=False, skip_group_check=True)

            def step(hb, n, par):
                g = hb * DS + n
                c_cast(hb, g, n)
                if isinstance(n, int) and n + LEAD >= DS:
                    if hb + 1 < HALVES:
                        b_cast(hb + 1, g + LEAD, n + LEAD - DS)
                else:
                    b_cast(hb, g + LEAD, n + LEAD)
                state_sum(g - 1, 1 - par)

            b_cast(0, 2, 2)
            c_cast(0, 0, 0)
            pe.wait_ge(s["zt_done"], 4)
            pe.wait_ge(s["a_done"], 2)
            open_sums(0)
            b_cast(0, 3, 3)
            for n in range(1, 6):
                step(0, n, n % 2)
                if n in (PROJ, DELTA, DELTA + 1):
                    pe.wait_ge(s["b_done"], n + LEAD + 1)
                if n == PROJ:
                    x_proj(1)
                    pe.wait_ge(s["hi_done"], 2)
                if n in (DELTA, DELTA + 1):
                    dt_proj(1, n - DELTA)
                    pe.wait_ge(s["sp_relu"], EC + n - DELTA + 1)
            with pe.Fori(3, DS // 2 - 2) as i:
                for par in range(2):
                    step(0, 2 * i + par, par)
            for n in range(DS - 4, DS):
                if n == DS - LEAD:
                    pe.wait_ge(s["stack_done"], 2)
                step(0, n, n % 2)
            c_cast(1, DS, 0)
            b_cast(1, DS + LEAD, LEAD)
            state_sum(DS - 1, 1, last=True)
            c_cast(1, DS + 1, 1)
            b_cast(1, DS + 1 + LEAD, 1 + LEAD)
            pe.wait_ge(s["y_used"], 1)
            open_sums(1)
            state_sum(DS, 0)

            def route(n):
                pe.wait_ge(s["b_done"], DS + n + LEAD + 1)
                if n in (TURN, TURN + 1):
                    turn_x1(0, n - TURN)
                    pe.wait_ge(s["xt_done"], n - TURN + 1)
                if n in (LOGIT, LOGIT + 1):
                    logits(0, n - LOGIT)
                    pe.wait_ge(s["lg_done"], n - LOGIT + 1)
                if n == COUNT:
                    counts(0)
                    pe.wait_ge(s["pos_done"], 1)

            for n in range(2, 6):
                step(1, n, n % 2)
                route(n)
            with pe.Fori(3, 5) as i:
                for par in range(2):
                    step(1, 2 * i + par, par)
            for n in range(10, DS):
                step(1, n, n % 2)
                if n == COUNT:
                    route(n)
            state_sum(2 * DS - 1, 1, last=True)

            turn_x1(1, 0)
            turn_x1(1, 1)
            logits(1, 0)
            logits(1, 1)
            pe.wait_ge(s["lg_done"], 4)
            counts(1)
            pe.wait_ge(s["pos_done"], 2)

            def split_mm(out_, hi_a, lo_a, hi_b, lo_b, start, stop):
                nc.tensor.matmul(out_, hi_a, hi_b, start=start, stop=False)
                nc.tensor.matmul(out_, hi_a, lo_b, start=False, stop=False)
                return nc.tensor.matmul(out_, lo_a, hi_b, start=False, stop=stop)

            def turn_rows(e):
                pe.wait_ge(s["xe_in"], 32 * (e + 1))
                for c in range(KC):
                    for t in range(ET):
                        ins = nc.tensor.transpose(ps[:, 6 + c, t * P:t * P + EROWS[t]],
                                                  xe[0:EROWS[t], t, c * P:(c + 1) * P],
                                                  cst[0:EROWS[t], CID:CID + EROWS[t]])
                ins.then_inc(s["xet_psum"], 1)

            def turn_results(e):
                pe.wait_ge(s["o_done"], e + 1)
                for t in range(ET):
                    for c in range(KC):
                        ins = nc.tensor.transpose(
                            ps[0:EROWS[t], 6 + t // 2, (t % 2) * DM + c * P:(t % 2) * DM + (c + 1) * P],
                            eot[:, c, t * P:t * P + EROWS[t]], ident)
                ins.then_inc(s["r_psum"], 1)

            def expert(e, first, last):
                pe.wait_ge(s["xthi_done"], e + 1)
                pe.wait_ge(s["xtlo_done"], e + 1)
                slots = bass.ds(e * CAP, CAP)
                for f in range(FC):
                    if f % FP == 0:
                        pe.wait_ge(s["w1hi_done"], WP * e + f // FP + 1)
                        pe.wait_ge(s["w1lo_done"], WP * e + f // FP + 1)
                    if f >= 4:
                        pe.wait_ge(s["htlo_done"], e * FC + f - 3)
                    fs = slice(f * P, (f + 1) * P)
                    for c in range(KC):
                        ins = split_mm(ps[:, f % 4, 0:CAP], w1hi[:, c, fs], w1lo[:, c, fs],
                                       xthi[:, c, slots], xtlo[:, c, slots], c == 0, c == KC - 1)
                    ins.then_inc(s["h_psum"], 1)
                    if f == FC // 2 - 1 and not first:
                        turn_results(e - 1)
                if not last:
                    if not first:
                        pe.wait_ge(s["r_act"], 2 * e)
                        pe.wait_ge(s["r_dve"], e)
                    turn_rows(e + 1)
                pe.wait_ge(s["o_done"], e)
                for f in range(FC):
                    if f % FP == 0:
                        pe.wait_ge(s["w2hi_done"], WP * e + f // FP + 1)
                        pe.wait_ge(s["w2lo_done"], WP * e + f // FP + 1)
                    pe.wait_ge(s["htlo_done"], e * FC + f + 1)
                    for c in range(KC):
                        cs = slice(c * P, (c + 1) * P)
                        ins = split_mm(ps[:, 4 + c, 0:CAP], w2hi[:, f, cs], w2lo[:, f, cs],
                                       hthi[:, f, :], htlo[:, f, :], f == 0, f == FC - 1)
                ins.then_inc(s["o_psum"], 1)

            turn_rows(0)
            expert(0, True, False)
            with pe.Fori(1, NE - 1) as e:
                expert(e, False, False)
            expert(NE - 1, False, True)
            pe.wait_ge(s["r_act"], 2 * (NE - 1))
            turn_results(NE - 1)

        @block.vector
        def _(dve):
            steps = [0]

            def link(ins):
                steps[0] += 1
                ins.then_inc(s["dve_step"], 1)
                dve.wait_ge(s["dve_step"], steps[0])

            dve.wait_ge(s["inp_in"], 16)
            dve.wait_ge(s["cw_in"], 16)
            nc.vector.tensor_tensor(cwb[:], cwb[:], inps[:, None, :].to_broadcast([P, TAPS, DI]), ALU.mult
                                    ).then_inc(s["cw_done"], 1)
            dve.wait_ge(s["x_in"], 16)
            for j in range(TILES):
                ins = nc.vector.bn_stats(stats[:, j, :], xnat[:, j, :])
            link(ins)
            for j in range(TILES):
                ins = nc.vector.bn_aggr(mvz[:, j, :], stats[:, j, :])
            link(ins)
            nc.vector.tensor_scalar(vz[:], mvz[:, :, 1], EPS, None, ALU.add).then_inc(s["z_stats"], 1)
            dve.wait_ge(s["z_rstd"], 1)
            nc.vector.scalar_tensor_tensor(out=nmz[:], in0=mvz[:, :, 0], scalar=-1.0, in1=rz[:],
                                           op0=ALU.mult, op1=ALU.mult).then_inc(s["z_scale"], 1)
            dve.wait_ge(s["wg_psum"], 1)
            nc.vector.scalar_tensor_tensor(
                out=wgs[:], in0=ps[:, 0:1, 0:NE].to_broadcast([P, KC, NE]), scalar=-1.0 / DM, in1=wgs[:],
                op0=ALU.mult, op1=ALU.add).then_inc(s["wg_done"], 1)

            def parts(hb):
                cols = halves(hb)
                dve.wait_ge(s["hi_done"], hb + 1)
                link(nc.vector.tensor_tensor(rest[:], rest[:], stack[:, cols], ALU.subtract))
                nc.vector.tensor_copy(stack[BC:2 * BC, cols], rest[BC:2 * BC, :])
                link(nc.vector.tensor_copy(stack[2 * BC:3 * BC, cols], rest[2 * BC:3 * BC, :]))
                nc.vector.tensor_tensor(stack[2 * BC:3 * BC, cols], rest[2 * BC:3 * BC, :],
                                        stack[2 * BC:3 * BC, cols], ALU.subtract
                                        ).then_inc(s["stack_done"], 1)

            def softplus(hb):
                for c in range(EC):
                    dve.wait_ge(s["sp_exp"], hb * EC + c + 1)
                    ins = nc.vector.tensor_scalar(delta[:, c, halves(hb)], spe[hb][:, c, :], 1.0, -1.0,
                                                  ALU.add, ALU.add)
                link(ins)
                for c in range(EC):
                    d = delta[:, c, halves(hb)]
                    dve.wait_ge(s["sp_sum"], hb * EC + c + 1)
                    ins = nc.vector.tensor_tensor(d, spr[hb][:, c, :], d, ALU.subtract)
                link(ins)
                for c in range(EC):
                    d = delta[:, c, halves(hb)]
                    dve.wait_ge(s["sp_ln"], hb * EC + c + 1)
                    nc.vector.tensor_tensor(d, spl[hb][:, c, :], d, ALU.add).then_inc(s["delta_done"], 1)

            def z_turned(m):
                dve.wait_ge(s["zt_psum"], m + 1)
                nc.vector.tensor_copy(zst[:, 2 * m:2 * m + 2, :], ps[:, m % 2, :]
                                      .rearrange("p (j d) -> p j d", j=2)).then_inc(s["zt_done"], 1)

            parts(0)
            dve.wait_ge(s["ch_in"], 16)
            dve.wait_ge(s["small_in"], 64)
            for c in range(EC):
                ins = nc.vector.tensor_scalar(diagd[:, c, :], ident, ch[:, c, DSK:DSK + 1], None, ALU.mult)
            ins.then_inc(s["a_done"], 1)
            nc.vector.tensor_copy(tri[:], cst[:, CTRI:CTRI + P])
            for j in range(TILES):
                nc.vector.tensor_copy(xrow[:, j, :, DM + 1], cst[:, CDST + TOPK * j:CDST + TOPK * (j + 1)])
            dve.wait_ge(s["a_exp"], 1)
            nc.vector.tensor_scalar(anegs[:], anegs[:], -1.0, None, ALU.mult).then_inc(s["a_done"], 1)
            for sl in range(2):
                if sl == 0:
                    dve.wait_ge(s["sp_relu"], EC)
                else:
                    dve.wait_ge(s["u_done"], EC * HALVES)
                nc.vector.memset(da[sl].rearrange("p c (b l) -> p (c b) l", l=L)[:, :, 0:1], 0.0
                                 ).then_inc(s["scan_done"], 1)
                if sl == 0:
                    softplus(0)
            dve.sem_inc(s["mult_done"], 2)
            for m in range(4):
                z_turned(m)

            def scan(g, par):
                dve.wait_ge(s["mult_done"], g + 1)
                dve.wait_ge(s["da_done"], EC * (g + 1))
                dve.wait_ge(s["dbu_done"], g + 3)
                nc.vector.tensor_tensor_scan(h[par][:].rearrange("p c t -> p (c t)"),
                                             da[par].rearrange("p c t -> p (c t)"),
                                             dbu[par][:].rearrange("p c t -> p (c t)"), 0.0,
                                             ALU.mult, ALU.add).then_inc(s["scan_done"], 1)

            def mult(g, par):
                dve.wait_ge(s["scan_done"], g + 3)
                dve.wait_ge(s["c_psum"], g + 1)
                dve.wait_ge(s["ysum_done"], g + 1)
                nc.vector.tensor_tensor(hc[par][:], h[par][:],
                                        ps[:, CBANK:CBANK + 1, :].to_broadcast([P, EC, HT]),
                                        ALU.mult).then_inc(s["mult_done"], 1)

            def steps_of(g0, lo, hi):
                with dve.Fori(lo, hi) as i:
                    scan(g0 + 2 * i + 1, 1)
                    mult(g0 + 2 * i, 0)
                    scan(g0 + 2 * i + 2, 0)
                    mult(g0 + 2 * i + 1, 1)

            def gate_y(hb, m):
                tiles = slice(hb * HTILES + 2 * m, hb * HTILES + 2 * m + 2)
                return nc.vector.tensor_tensor(x1[:, tiles, :], y[:, 2 * m:2 * m + 2, :], zst[:, tiles, :],
                                               ALU.mult)

            def add_x(hb, m):
                tiles = slice(hb * HTILES + 2 * m, hb * HTILES + 2 * m + 2)
                nc.vector.tensor_tensor(x1[:, tiles, :], x1[:, tiles, :], xnat[:, tiles, :], ALU.add
                                        ).then_inc(s["x1_done"], 1)

            def variance(hb):
                tiles = slice(hb * HTILES, (hb + 1) * HTILES)
                dve.wait_ge(s["x1_done"], 2 * hb + 2)
                for j in range(hb * HTILES, (hb + 1) * HTILES):
                    ins = nc.vector.bn_stats(stats[:, j, :], x1[:, j, :])
                link(ins)
                for j in range(hb * HTILES, (hb + 1) * HTILES):
                    ins = nc.vector.bn_aggr(mvx[:, j, :], stats[:, j, :])
                link(ins)
                nc.vector.tensor_scalar(vx[:, tiles], mvx[:, tiles, 1], EPS, None, ALU.add
                                        ).then_inc(s["ln_var"], 1)

            def choose(hb):
                tiles = slice(hb * HTILES, (hb + 1) * HTILES)
                js = range(hb * HTILES, (hb + 1) * HTILES)
                dve.wait_ge(s["ln_rstd"], hb + 1)
                nc.vector.scalar_tensor_tensor(out=nmx[:, tiles], in0=mvx[:, tiles, 0], scalar=-1.0,
                                               in1=rx[:, tiles], op0=ALU.mult, op1=ALU.mult
                                               ).then_inc(s["ln_scale"], 1)
                dve.wait_ge(s["lg_done"], 2 * hb + 2)
                link(nc.vector.tensor_tensor(lg[:, tiles, :], lg[:, tiles, :],
                                             rx[:, tiles, None].to_broadcast([P, HTILES, NE]), ALU.mult))
                for j in js:
                    ins = nc.vector.max(top[:, j, :], lg[:, j, :])
                link(ins)
                for j in js:
                    ins = nc.vector.max_index(topi[:, j, :], top[:, j, :], lg[:, j, :])
                link(ins)
                link(nc.vector.tensor_copy(topf[:, tiles, :], topi[:, tiles, 0:TOPK]))
                link(nc.vector.tensor_tensor(
                    oh[:, tiles, :, :],
                    cst[:, None, None, CIOTA:CIOTA + NE].to_broadcast([P, HTILES, TOPK, NE]),
                    topf[:, tiles, :, None].to_broadcast([P, HTILES, TOPK, NE]), ALU.is_equal))
                nc.vector.tensor_tensor(multi[:, tiles, :], oh[:, tiles, 0, :], oh[:, tiles, 1, :], ALU.add
                                        ).then_inc(s["multi_done"], 1)
                nc.vector.tensor_tensor(etop[:, tiles, :], top[:, tiles, :],
                                        top[:, tiles, 0:1].to_broadcast([P, HTILES, NE]), ALU.subtract
                                        ).then_inc(s["top_sub"], 1)

            def place(hb):
                tiles = slice(hb * HTILES, (hb + 1) * HTILES)
                dve.wait_ge(s["top_exp"], hb + 1)
                link(nc.vector.tensor_reduce(rsum[:, tiles], etop[:, tiles, :], AX.X, ALU.add))
                link(nc.vector.reciprocal(rsum[:, tiles], rsum[:, tiles]))
                nc.vector.tensor_tensor(xrow[:, tiles, :, DM], etop[:, tiles, 0:TOPK],
                                        rsum[:, tiles, None].to_broadcast([P, HTILES, TOPK]), ALU.mult
                                        ).then_inc(s["gates_done"], 1)
                dve.wait_ge(s["pos_done"], hb + 1)
                link(nc.vector.tensor_tensor(ohc[:, tiles, :, :], oh[:, tiles, :, :],
                                             cum[:, :, None, :].to_broadcast([P, HTILES, TOPK, NE]), ALU.mult))
                link(nc.vector.tensor_reduce(pos[:, tiles, :], ohc[:, tiles, :, :], AX.X, ALU.add))
                link(nc.vector.scalar_tensor_tensor(out=slot[:, tiles, :], in0=topf[:, tiles, :],
                                                    scalar=float(CAP), in1=pos[:, tiles, :],
                                                    op0=ALU.mult, op1=ALU.add))
                link(nc.vector.tensor_scalar(pos[:, tiles, :], pos[:, tiles, :], float(CAP), DROPPED,
                                             ALU.is_ge, ALU.mult))
                nc.vector.tensor_tensor(sloti[:, tiles, :], slot[:, tiles, :], pos[:, tiles, :], ALU.add
                                        ).then_inc(s["slots_done"], 1)

            scan(0, 0)
            steps_of(0, 0, 2)
            parts(1)
            steps_of(0, 2, 4)
            softplus(1)
            steps_of(0, 4, DS // 2 - 1)
            scan(DS - 1, 1)
            mult(DS - 2, 0)
            scan(DS, 0)
            mult(DS - 1, 1)
            scan(DS + 1, 1)
            mult(DS, 0)
            dve.wait_ge(s["ysum_done"], DS + 2)
            gate_y(0, 0)
            gate_y(0, 1).then_inc(s["y_used"], 1)
            dve.wait_ge(s["y_used"], 1)
            add_x(0, 0)
            add_x(0, 1)
            scan(DS + 2, 0)
            mult(DS + 1, 1)
            variance(0)
            steps_of(DS, 1, 4)
            choose(0)
            steps_of(DS, 4, 6)
            place(0)
            steps_of(DS, 6, DS // 2 - 1)
            scan(2 * DS - 1, 1)
            mult(2 * DS - 2, 0)
            mult(2 * DS - 1, 1)
            dve.wait_ge(s["ysum_done"], HALVES * DS + 2)
            gate_y(1, 0)
            link(gate_y(1, 1))
            add_x(1, 0)
            add_x(1, 1)
            variance(1)
            choose(1)
            place(1)

            def low_w1(e, m):
                cols = slice(m * FP * P, (m + 1) * FP * P)
                dve.wait_ge(s["w1hi_done"], WP * e + m + 1)
                nc.vector.tensor_tensor(w1lo[:, :, cols], w1raw[:, :, cols], w1hi[:, :, cols].bitcast(F32),
                                        ALU.subtract).then_inc(s["w1lo_done"], 1)

            def rows_lo(e):
                slots = bass.ds(e * CAP, CAP)
                dve.wait_ge(s["xe_in"], 32 * (e + 1))
                for t0, t1, rows in ((0, 2, P), (2, 3, EROWS[2])):
                    tiles = bass.ds(e * ET + t0, t1 - t0)
                    nc.vector.tensor_copy(gates[0:rows, tiles, :], xe[0:rows, t0:t1, DM:DM + 1])
                    nc.vector.tensor_copy(dst[0:rows, tiles, :], xe[0:rows, t0:t1, DM + 1:ROW]
                                          ).then_inc(s["meta_done"], 1)
                dve.wait_ge(s["xthi_done"], e + 1)
                nc.vector.tensor_tensor(xtlo[:, :, slots], ps[:, 6:8, 0:CAP], xthi[:, :, slots].bitcast(F32),
                                        ALU.subtract).then_inc(s["xtlo_done"], 1)

            def hidden_lo(e, f):
                dve.wait_ge(s["hthi_done"], e * FC + f + 1)
                nc.vector.scalar_tensor_tensor(out=htlo[:, f, :], in0=ps[:, f % 4, 0:CAP], scalar=0.0,
                                               in1=hthi[:, f, :].bitcast(F32), op0=ALU.max,
                                               op1=ALU.subtract).then_inc(s["htlo_done"], 1)

            def gated_rows(e):
                t = ET - 1
                dve.wait_ge(s["r_psum"], e + 1)
                dve.wait_ge(s["res_out"], 16 * ET * e)
                nc.vector.tensor_scalar(eo[0:EROWS[t], t, :], ps[0:EROWS[t], 7, 0:DM],
                                        gates[0:EROWS[t], bass.ds(e * ET + t, 1), 0], None, ALU.mult
                                        ).then_inc(s["r_dve"], 1)

            def expert(e, first, last):
                for f in range(FC):
                    hidden_lo(e, f)
                    if f == FC // 2 + 1 and not first:
                        gated_rows(e - 1)
                if not last:
                    rows_lo(e + 1)
                    for m in range(WP):
                        low_w1(e + 1, m)

            for m in range(WP):
                low_w1(0, m)
            rows_lo(0)
            expert(0, True, False)
            with dve.Fori(1, NE - 1) as e:
                expert(e, False, False)
            expert(NE - 1, False, True)
            gated_rows(NE - 1)
            for q in range(4):
                tiles = slice(2 * q, 2 * q + 2)
                dve.wait_ge(s[f"res_in{q}"], 32)
                link(nc.vector.tensor_tensor(x1[:, tiles, :], x1[:, tiles, :], resl[:, 0, tiles, :], ALU.add))
                nc.vector.tensor_tensor(x1[:, tiles, :], x1[:, tiles, :], resl[:, 1, tiles, :], ALU.add
                                        ).then_inc(s["sum_done"], 1)


def kernel(x, ctx_1024, L0_xattn_in_proj_w, L0_xattn_conv_w, L0_xattn_conv_b, L0_xattn_x_proj_w,
           L0_xattn_dt_proj_w, L0_xattn_dt_proj_b, L0_xattn_A_log, L0_xattn_D, L0_ffn_Wg, L0_ffn_w1,
           L0_ffn_w2):
    import ml_dtypes
    from concourse import bacc
    from concourse.bass_utils import run_bass_kernel_spmd

    def by_chunk(a):
        a = np.asarray(a)
        return a.reshape(a.shape[0] // P, P, -1).transpose(1, 0, 2)

    x_proj = np.asarray(L0_xattn_x_proj_w).T
    chan = np.concatenate([np.asarray(a).reshape(DI, -1) for a in (
        L0_xattn_conv_b, L0_xattn_dt_proj_b, L0_xattn_D, L0_xattn_A_log)], axis=1)
    consts = np.zeros((P, NCONST), np.float32)
    consts[:, CID:CID + P] = np.eye(P)
    consts[:, CTRI:CTRI + P] = np.triu(np.ones((P, P)), 1)
    for j in range(TILES):
        for k in range(TOPK):
            consts[:, CDST + TOPK * j + k] = k * T + j * P + np.arange(P)
    consts[:, CIOTA:CIOTA + NE] = np.arange(NE)
    sel = np.zeros((3, BC, BC, P), ml_dtypes.bfloat16)
    for n in range(BC):
        sel[:, n, n, :] = 1.0

    arrays = {
        "x": by_chunk(np.asarray(x).reshape(T, DM)),
        "ctx_t": np.asarray(ctx_1024).reshape(T, DC).T,
        "inproj_t": np.asarray(L0_xattn_in_proj_w).T,
        "xproj_t": by_chunk(np.concatenate([x_proj[:, DR:]] * 3 + [x_proj[:, 0:DR]], axis=1)),
        "dtproj_t": np.asarray(L0_xattn_dt_proj_w).T,
        "conv_w": np.asarray(L0_xattn_conv_w).reshape(DI, TAPS).T,
        "chan": by_chunk(chan),
        "wg": by_chunk(L0_ffn_Wg),
        "w1": np.asarray(L0_ffn_w1).reshape(NE, KC, P, DFF).transpose(0, 2, 1, 3),
        "w2": np.asarray(L0_ffn_w2).reshape(NE, FC, P, DM).transpose(0, 2, 1, 3),
        "consts": consts,
        "sel": sel.reshape(3 * BC, BC * P),
    }
    nc = bacc.Bacc("TRN2", target_bir_lowering=False, num_devices=1)
    ins, feed = {}, {}
    for name, a in arrays.items():
        a = np.ascontiguousarray(a)
        feed["in_" + name] = a
        ins[name] = nc.dram_tensor("in_" + name, a.shape, mybir.dt.from_np(a.dtype), kind="ExternalInput").ap()
    out = nc.dram_tensor("out", [T, DM], F32, kind="ExternalOutput").ap()
    build(nc, out=out, **ins)
    r = run_bass_kernel_spmd(nc, [feed], core_ids=[0])
    return r.results[0]["out"].reshape(B, L, DM)
```

```python
from contextlib import ExitStack

import numpy as np

import concourse.bass as bass
from concourse import mybir

F32 = mybir.dt.float32
F32R = mybir.dt.float32r
BF16 = mybir.dt.bfloat16
U32 = mybir.dt.uint32
ALU = mybir.AluOpType
ACT = mybir.ActivationFunctionType
AX = mybir.AxisListType

P = 128
B, L, DM = 4, 256, 256
DC = 128
DI, DS, TAPS, DR = 256, 16, 4, 8
EC = DI // P
T = B * L
TILES = T // P
HALVES = 2
HT = T // HALVES
HTILES = HT // P
HB = B // HALVES
NE, TOPK, DFF = 8, 2, 1024
CAP = (5 * T * TOPK // NE + 3) // 4
SLOTS = NE * CAP
ET = (CAP + P - 1) // P
EROWS = [min(P, CAP - t * P) for t in range(ET)]
FC = DFF // P
KC = DM // P
ROW = DM + 2
DROPPED = 8192.0
EPS = 1e-5
CB, DTB, DSK, ALOG, NCH = 0, 1, 2, 3, 3 + DS
CID, CTRI, CDST = 0, P, 2 * P
CIOTA = CDST + TILES
NCONST = CIOTA + NE
BC = 2 * DS
XPC = 3 * BC + DR
WP = 4
FP = FC // WP
RING = 4
SUMS = 2
AHEAD = RING + 1
PROJ, DELTA, ZTURN, TURN, LOGIT, COUNT = 4, 6, 9, 2, 4, 9
W1_LATER = 4
SILU = RING + 1


def halves(hb):
    return slice(hb * HT, (hb + 1) * HT)


def build(nc, x, ctx_t, inproj_t, xproj_t, dtproj_t, conv_w, chan, wg, w1, w2, consts, slot_numbers, sel,
          out):
    xe_dram = nc.dram_tensor("expert_rows", [SLOTS, ROW], F32, kind="Internal").ap()

    with ExitStack() as ctx:
        def alloc(stack, name, shape, dt=F32):
            return stack.enter_context(nc.sbuf_tensor(name, shape, dt))

        def sb(name, shape, dt=F32):
            return alloc(ctx, name, shape, dt)

        cst = sb("cst", [P, NCONST])
        ident = cst[:, CID:CID + P]
        ch = sb("ch", [P, EC, NCH])
        x1 = sb("x1", [P, TILES, DM])
        wgs = sb("wgs", [P, KC, NE])
        w1raw = sb("w1raw", [P, KC, DFF])
        w2raw = sb("w2raw", [P, FC, DM])
        w1hi = sb("w1hi", [P, KC, DFF], F32R)
        w1lo = sb("w1lo", [P, KC, DFF], F32R)
        anegs = sb("anegs", [P, EC, DS])
        diagd = sb("diagd", [P, EC, P])
        tri = sb("tri", [P, P], BF16)
        ones = sb("ones", [P, P], BF16)
        onesf = sb("onesf", [P, P])
        fill = sb("fill", [P, ROW])
        nhalf = sb("nhalf", [P, TILES])
        stats = sb("stats", [P, TILES, 6])
        mvz = sb("mvz", [P, TILES, 2])
        mvx = sb("mvx", [P, TILES, 2])
        vz = sb("vz", [P, TILES])
        rz = sb("rz", [P, TILES])
        nmz = sb("nmz", [P, TILES])
        vx = sb("vx", [P, TILES])
        rx = sb("rx", [P, TILES])
        nmx = sb("nmx", [P, TILES])
        lg = sb("lg", [P, TILES, NE])
        top = sb("top", [P, TILES, NE])
        etop = sb("etop", [P, TILES, NE])
        topi = sb("topi", [P, TILES, NE], U32)
        topf = sb("topf", [P, TILES, TOPK])
        rsum = sb("rsum", [P, TILES])
        oh = sb("oh", [P, TILES, TOPK, NE])
        ohc = sb("ohc", [P, TILES, TOPK, NE])
        cum = sb("cum", [P, HTILES, NE])
        multi = sb("multi", [P, TILES, NE], BF16)
        pos = sb("pos", [P, TILES, TOPK])
        slot = sb("slot", [P, TILES, TOPK])
        key = sb("key", [P, HTILES])
        sloti = sb("sloti", [P, TILES, TOPK], U32)
        gates = sb("gates", [P, NE * ET, 1])
        dst = sb("dst", [P, NE * ET, 1], U32)
        xe = sb("xe", [P, ET, ROW])
        xrow = sb("xrow", [P, TILES, TOPK, ROW])
        meta0 = sb("meta0", [P, ET, 2])
        numbers = sb("numbers", [P, CAP])

        scan_mem = ExitStack()

        def sm(name, shape, dt=F32):
            return alloc(scan_mem, name, shape, dt)

        proj = sm("proj", [P, (1 + TAPS) * DI])
        xnat = sm("xnat", [P, TILES, DM])
        zst = sm("zst", [P, TILES, DM])
        ctxs = sm("ctxs", [P, T])
        xps = sm("xps", [P, EC, XPC])
        dtps = sm("dtps", [3 * BC + DR, DI])
        dtlo = sm("dtlo", [3 * BC + DR, T])
        u = sm("u", [P, EC, T])
        delta = sm("delta", [P, EC, T])
        du = sm("du", [P, EC, T])
        sels = sm("sels", [3 * BC, BC * P], BF16)
        stack = sm("stack", [3 * BC, T], BF16)
        rest = sm("rest", [3 * BC, HT])
        spr = [sm(f"spr{i}", [P, EC, HT]) for i in range(HALVES)]
        bsb = [sm(f"bsb{i}", [P, HT]) for i in range(RING)]
        dbu = [sm(f"dbu{i}", [P, EC, HT]) for i in range(RING)]
        da = [sm(f"da{i}", [P, EC, HT]) for i in range(RING)]
        h = [sm(f"h{i}", [P, EC, HT]) for i in range(RING)]
        hc = [sm(f"hc{i}", [P, EC, HT]) for i in range(2)]
        inps = proj[:, 0:DI]
        cwb = proj[:, DI:].rearrange("p (k d) -> p k d", d=DI)
        takes = proj[:, 0:HTILES * CAP].rearrange("p (t n) -> p t n", n=CAP)
        zs = w2raw
        spe, spl = [hc[0], w1raw[:, 0, :]], [dbu[0], w1raw[:, 1, :]]
        spe[1], spl[1] = [a.rearrange("p (c t) -> p c t", c=EC) for a in (spe[1], spl[1])]
        xnt = spr[0]
        scan_mem.close()

        w2hi = sb("w2hi", [P, FC, DM], F32R)
        w2lo = sb("w2lo", [P, FC, DM], F32R)
        xthi = sb("xthi", [P, KC, SLOTS], F32R)
        xtlo = sb("xtlo", [P, KC, SLOTS], F32R)
        hthi = sb("hthi", [P, FC, CAP], F32R)
        htlo = sb("htlo", [P, FC, CAP], F32R)
        eot = sb("eot", [P, KC, CAP])
        eo = sb("eo", [P, ET, DM])
        so_far = sb("so_far", [P, ET, DM])

        ps = ctx.enter_context(nc.psum_tensor("ps", [P, 8, HT], F32))
        y = ps[:, 0:2, :].rearrange("p b (t e) -> p (b t) e", e=DI)
        WORK, CBANK, BBANK = 2, 4, 6
        PBANK, DBANK = [BBANK, WORK], [WORK, WORK + 1, WORK + 1, WORK]

        s = {n: ctx.enter_context(nc.semaphore(n)) for n in (
            "ctx_in0 ctx_in1 inp_in x_in small_in sel_in w1_in w2_in xe_in fill_made xe_filled "
            "z_stats z_rstd z_scale zs_done zt_psum zt_done wg_psum wg_done "
            "cw_in ch_in cw_done conv_psum u_done xp_psum dtlo_done hi_done stack_done "
            "dt_psum sp_abs sp_exp sp_relu sp_sum sp_ln delta_done du_done a_exp a_done "
            "b_psum first_dbu b_done c_psum da_done scan_done dbu_done mult_done ysum_done "
            "y_half y_used x1_done ln_var ln_rstd ln_scale xn_done xt_psum xt_done lg_psum lg_done top_sub top_exp "
            "multi_done pos_psum pos_done gates_done slots_done scattered0 scattered1 takes_done numbers_in meta_in "
            "w1hi_done w1lo_done w2hi_done w2lo_done xet_psum xthi_done xtlo_done meta_done "
            "h_psum hthi_done htlo_done o_psum o_done r_psum so_far_set so_far_in0 so_far_in1 so_far_in2 r_done res_out x1_out dve_step").split()}

        block = ctx.enter_context(nc.Block())

        @block.sync
        def _(sp):
            sp.dma_start(inps, inproj_t).then_inc(s["inp_in"], 16)
            for hb in range(HALVES):
                sp.dma_start(ctxs[:, halves(hb)], ctx_t[:, halves(hb)]).then_inc(s[f"ctx_in{hb}"], 16)
            sp.dma_start(xnat[:], x).then_inc(s["x_in"], 16)
            sp.dma_start(cst[:], consts).then_inc(s["small_in"], 16)
            sp.dma_start(dtps[3 * BC:3 * BC + DR, :], dtproj_t).then_inc(s["small_in"], 16)
            sp.dma_start(wgs[:], wg).then_inc(s["small_in"], 16)
            sp.dma_start(sels[:], sel).then_inc(s["sel_in"], 16)
            sp.wait_ge(s["fill_made"], 1)
            sp.dma_start(xe_dram.rearrange("(t p) r -> p t r", p=P),
                         fill[:, None, :].to_broadcast([P, SLOTS // P, ROW])).then_inc(s["xe_filled"], 16)
            sp.wait_ge(s["delta_done"], EC * HALVES)
            sp.dma_start(w1raw[:], w1[0]).then_inc(s["w1_in"], 16)
            sp.wait_ge(s["zt_psum"], TILES // 2)
            sp.dma_start(w2raw[:], w2[0]).then_inc(s["w2_in"], 16)

            def rows_in(e):
                sp.dma_start(xe[:, 0:2, :], xe_dram[e * CAP:e * CAP + 2 * P].rearrange("(t p) r -> p t r", p=P)).then_inc(s["xe_in"], 16)
                sp.dma_start(xe[0:EROWS[2], 2, :], xe_dram[e * CAP + 2 * P:(e + 1) * CAP]).then_inc(s["xe_in"], 16)

            sp.dma_start(numbers[:], slot_numbers).then_inc(s["numbers_in"], 16)
            sp.wait_ge(s["scattered0"], 16 * HTILES * TOPK)
            rows_in(0)
            for hb in range(HALVES):
                sp.wait_ge(s["x1_done"], 2 * hb + 2)
                sp.dma_start(out[halves(hb)].rearrange("(t p) d -> p t d", p=P),
                             x1[:, hb * HTILES:(hb + 1) * HTILES, :]).then_inc(s["x1_out"], 16)
            for e in range(1, NE):
                if e == 1:
                    sp.wait_ge(s["scattered1"], 16 * HTILES * TOPK)
                    sp.dma_start(meta0[:, 0:2, :], xe_dram[0:2 * P, DM:ROW].rearrange("(t p) r -> p t r", p=P)
                                 ).then_inc(s["meta_in"], 16)
                    sp.dma_start(meta0[0:EROWS[2], 2, :], xe_dram[2 * P:CAP, DM:ROW]
                                 ).then_inc(s["meta_in"], 16)
                sp.wait_ge(s["xet_psum"], e - 1 + KC)
                if e > 1:
                    sp.wait_ge(s["meta_done"], 2 * e)
                rows_in(e)
                sp.wait_ge(s["w1hi_done"], WP * e)
                sp.wait_ge(s["w1lo_done"], WP * e)
                sp.wait_ge(s["h_psum"], FC * (e - 1) + W1_LATER)
                sp.dma_start(w1raw[:], w1[e]).then_inc(s["w1_in"], 16)
                sp.wait_ge(s["w2hi_done"], WP * e)
                sp.wait_ge(s["w2lo_done"], WP * e)
                sp.dma_start(w2raw[:], w2[e]).then_inc(s["w2_in"], 16)
            sp.wait_ge(s["x1_out"], 16 * HALVES)
            sp.wait_ge(s["res_out"], 16 * NE * ET)

        @block.gpsimd
        def _(pool):
            nc.gpsimd.memset(onesf[:], 1.0)
            nc.gpsimd.memset(ones[:], 1.0)
            nc.gpsimd.memset(nhalf[:], -0.5)
            nc.gpsimd.memset(fill[:, 0:DM + 1], 0.0)
            nc.gpsimd.memset(fill[:, DM + 1:ROW], DROPPED).then_inc(s["fill_made"], 1)
            pool.sem_inc(s["dbu_done"], RING + 2)
            pool.wait_ge(s["z_stats"], 1)
            pool.wait_ge(s["fill_made"], 1)
            nc.gpsimd.tensor_tensor(rz[:], vz[:], nhalf[:], ALU.pow).then_inc(s["z_rstd"], 1)
            def max_plus_exp(hb, chunks):
                for c in chunks:
                    pool.wait_ge(s["sp_relu"], hb * EC + c + 1)
                    pool.wait_ge(s["sp_exp"], hb * EC + c + 1)
                    nc.gpsimd.tensor_tensor(spr[hb][:, c, :], spr[hb][:, c, :], spe[hb][:, c, :], ALU.add
                                            ).then_inc(s["sp_sum"], 1)

            def delta_u(hb, chunks):
                for c in chunks:
                    pool.wait_ge(s["delta_done"], EC * hb + c + 1)
                    nc.gpsimd.tensor_tensor(du[:, c, halves(hb)], delta[:, c, halves(hb)],
                                            u[:, c, halves(hb)], ALU.mult).then_inc(s["du_done"], 1)

            def step(hb, g, r):
                pool.wait_ge(s["b_done"], g + 1)
                pool.wait_ge(s["scan_done"], g + 1)
                nc.gpsimd.tensor_tensor(dbu[r][:], du[:, :, halves(hb)],
                                        bsb[r][:, None, :].to_broadcast([P, EC, HT]), ALU.mult
                                        ).then_inc(s["dbu_done"], 1)

            def steps(hb, lo, hi):
                with pool.Fori(lo, hi) as i:
                    for r in range(RING):
                        step(hb, RING * i + r, r)

            def row_rstd(hb):
                tiles = slice(hb * HTILES, (hb + 1) * HTILES)
                pool.wait_ge(s["ln_var"], hb + 1)
                nc.gpsimd.tensor_tensor(rx[:, tiles], vx[:, tiles], nhalf[:, tiles], ALU.pow
                                        ).then_inc(s["ln_rstd"], 1)

            def send(hb):
                pool.wait_ge(s["gates_done"], hb + 1)
                pool.wait_ge(s["slots_done"], hb + 1)
                for j in range(hb * HTILES, (hb + 1) * HTILES):
                    pool.wait_ge(s["xn_done"], j + 1)
                    for k in range(TOPK):
                        nc.gpsimd.indirect_dma_start(
                            xe_dram, bass.IndirectOffsetOnAxis(ap=sloti[:, j, k:k + 1], axis=0),
                            xrow[:, j, k, :], None, bounds_check=SLOTS - 1, oob_is_err=False
                        ).then_inc(s[f"scattered{hb}"], 16)

            max_plus_exp(0, range(EC))
            delta_u(0, [0])
            pool.wait_ge(s["du_done"], EC)
            for g in range(2, RING):
                step(0, g, g)
            steps(0, 1, 3)
            for g in range(3 * RING, DS):
                step(0, g, g % RING)
                if g - 3 * RING < EC:
                    max_plus_exp(1, [g - 3 * RING])
            delta_u(1, range(EC))
            pool.wait_ge(s["du_done"], EC * HALVES)
            steps(1, 4, 6)
            row_rstd(0)
            steps(1, 6, 8)
            pool.wait_ge(s["xe_filled"], 16)
            send(0)
            row_rstd(1)
            pool.wait_ge(s["xe_in"], 32)
            send(1)

            def low_w2(e, m):
                fs = slice(m * FP, (m + 1) * FP)
                pool.wait_ge(s["w2hi_done"], WP * e + m + 1)
                nc.gpsimd.tensor_tensor(w2lo[:, fs, :], w2raw[:, fs, :], w2hi[:, fs, :].bitcast(F32),
                                        ALU.subtract).then_inc(s["w2lo_done"], 1)

            def fetch(e):
                pool.wait_ge(s["meta_done"], 2 * (e + 1))
                if e >= 1:
                    pool.wait_ge(s["res_out"], 16 * ET * e)
                for t in range(ET):
                    nc.gpsimd.indirect_dma_start(
                        so_far[0:EROWS[t], t, :], None, out,
                        bass.IndirectOffsetOnAxis(ap=dst[0:EROWS[t], e * ET + t, :], axis=0),
                        bounds_check=T - 1, oob_is_err=False).then_inc(s[f"so_far_in{t}"], 16)

            def send_results(e):
                for t in range(ET):
                    pool.wait_ge(s["r_done"], ET * e + t + 1)
                    nc.gpsimd.indirect_dma_start(
                        out, bass.IndirectOffsetOnAxis(ap=dst[0:EROWS[t], e * ET + t, :], axis=0),
                        eo[0:EROWS[t], t, :], None, bounds_check=T - 1, oob_is_err=False
                    ).then_inc(s["res_out"], 16)

            pool.wait_ge(s["xthi_done"], KC)
            nc.gpsimd.memset(so_far[:], 0.0).then_inc(s["so_far_set"], 1)
            pool.wait_ge(s["so_far_set"], 1)
            pool.wait_ge(s["x1_out"], 16 * HALVES)
            for e in range(NE):
                pool.wait_ge(s["w2_in"], 16 * (e + 1))
                for m in range(WP // 2 if e == NE - 1 else WP):
                    low_w2(e, m)
                    if m == WP // 2 - 1 and e >= 1:
                        send_results(e - 1)
                fetch(e)
            send_results(NE - 1)

        @block.scalar
        def _(act):
            act.dma_start(cwb, conv_w[None, :, :].to_broadcast([P, TAPS, DI])).then_inc(s["cw_in"], 16)
            act.dma_start(ch[:], chan).then_inc(s["ch_in"], 16)
            act.dma_start(xps[:], xproj_t).then_inc(s["small_in"], 16)

            def conv_silu(hb):
                for c in range(EC):
                    act.wait_ge(s["conv_psum"], hb * EC + c + 1)
                    nc.scalar.activation(u[:, c, halves(hb)], ps[:, WORK + c, :], ACT.Silu,
                                         bias=ch[:, c, CB:CB + 1]).then_inc(s["u_done"], 1)

            def parts(hb):
                act.wait_ge(s["xp_psum"], hb + 1)
                nc.scalar.activation(dtlo[3 * BC:3 * BC + DR, halves(hb)],
                                     ps[3 * BC:3 * BC + DR, PBANK[hb], :], ACT.Copy
                                     ).then_inc(s["dtlo_done"], 1)
                if hb:
                    act.wait_ge(s["stack_done"], hb)
                    nc.scalar.activation(rest[:], ps[0:3 * BC, PBANK[hb], :], ACT.Copy)
                nc.scalar.activation(stack[:, halves(hb)], ps[0:3 * BC, PBANK[hb], :], ACT.Copy
                                     ).then_inc(s["hi_done"], 1)

            def z_silu(tiles):
                for j in tiles:
                    ins = nc.scalar.activation(zs[:, j, :], xnat[:, j, :], ACT.Silu,
                                               bias=nmz[:, j:j + 1], scale=rz[:, j:j + 1])
                ins.then_inc(s["zs_done"], 1)

            def exps(hb, c):
                q = hb * EC + c
                v = ps[:, DBANK[q], :]
                act.wait_ge(s["dt_psum"], q + 1)
                nc.scalar.activation(spe[hb][:, c, :], v, ACT.Abs, bias=ch[:, c, DTB:DTB + 1]
                                     ).then_inc(s["sp_abs"], 1)
                if hb:
                    nc.scalar.activation(spr[hb][:, c, :], v, ACT.Relu, bias=ch[:, c, DTB:DTB + 1]
                                         ).then_inc(s["sp_relu"], 1)
                act.wait_ge(s["sp_abs"], q + 1)
                nc.scalar.activation(spe[hb][:, c, :], spe[hb][:, c, :], ACT.Exp, scale=-1.0
                                     ).then_inc(s["sp_exp"], 1)

            def logs(hb):
                for c in range(EC):
                    act.wait_ge(s["sp_exp"], hb * EC + c + 1)
                    nc.scalar.activation(spl[hb][:, c, :], spe[hb][:, c, :], ACT.Ln, bias=1.0
                                         ).then_inc(s["sp_ln"], 1)

            act.wait_ge(s["ch_in"], 16)
            conv_silu(0)
            act.wait_ge(s["z_scale"], 1)
            z_silu(range(2))
            parts(0)
            nc.scalar.activation(anegs[:], ch[:, :, ALOG:ALOG + DS], ACT.Exp).then_inc(s["a_exp"], 1)
            for c in range(EC):
                exps(0, c)
            logs(0)

            def z_turned(m):
                act.wait_ge(s["zt_psum"], m + 1)
                nc.scalar.activation(zst[:, 2 * m:2 * m + 2, :],
                                     ps[:, WORK + m % 2, :].rearrange("p (j d) -> p j d", j=2), ACT.Copy
                                     ).then_inc(s["zt_done"], 1)

            def b_copy(g):
                act.wait_ge(s["b_psum"], g + 1)
                act.wait_ge(s["dbu_done"], g + 1)
                if RING <= g < RING + 2:
                    act.wait_ge(s["first_dbu"], g - RING + 1)
                nc.scalar.activation(bsb[g % RING][:], ps[:, BBANK + g % SUMS, :], ACT.Copy
                                     ).then_inc(s["b_done"], 1)

            copied = [0]

            def b_copies(last):
                while copied[0] <= min(last, HALVES * DS - 1):
                    b_copy(copied[0])
                    copied[0] += 1

            def decay(g):
                hb, n = g // DS, g % DS
                act.wait_ge(s["scan_done"], g + 1)
                for c in range(EC):
                    if n == 0:
                        act.wait_ge(s["delta_done"], EC * hb + c + 1)
                    nc.scalar.activation(
                        da[g % RING][:, c, :].rearrange("p (b l) -> p b l", b=HB)[:, :, 1:L],
                        delta[:, c, halves(hb)].rearrange("p (b l) -> p b l", b=HB)[:, :, 1:L],
                        ACT.Exp, scale=anegs[:, c, n:n + 1]).then_inc(s["da_done"], 1)

            def x1_turned(hb, m):
                act.wait_ge(s["xt_psum"], 2 * hb + m + 1)
                nc.scalar.activation(xnt[:, :, m * 2 * P:(m + 1) * 2 * P],
                                     ps[:, WORK + m, :].rearrange("p (c t) -> p c t", c=KC),
                                     ACT.Copy).then_inc(s["xt_done"], 1)

            def logits_out(hb, m):
                act.wait_ge(s["lg_psum"], 2 * hb + m + 1)
                nc.scalar.activation(lg[:, hb * HTILES + 2 * m:hb * HTILES + 2 * m + 2, :],
                                     ps[:, WORK + m, 0:2 * NE].rearrange("p (t e) -> p t e", e=NE),
                                     ACT.Copy).then_inc(s["lg_done"], 1)

            def counts_out(hb):
                act.wait_ge(s["pos_psum"], hb + 1)
                nc.scalar.activation(cum[:], ps[:, WORK, 0:HTILES * NE].rearrange("p (t e) -> p t e", e=NE),
                                     ACT.Copy).then_inc(s["pos_done"], 1)

            def normalise(j):
                act.wait_ge(s["ln_scale"], j // HTILES + 1)
                nc.scalar.activation(xrow[:, j, :, 0:DM],
                                     x1[:, j:j + 1, :].to_broadcast([P, TOPK, DM]), ACT.Identity,
                                     bias=nmx[:, j:j + 1], scale=rx[:, j:j + 1]).then_inc(s["xn_done"], 1)

            def top_exp(hb):
                act.wait_ge(s["top_sub"], hb + 1)
                tiles = slice(hb * HTILES, (hb + 1) * HTILES)
                nc.scalar.activation(etop[:, tiles, :], etop[:, tiles, :], ACT.Exp).then_inc(s["top_exp"], 1)

            def split_w1(e, m):
                cols = slice(m * FP * P, (m + 1) * FP * P)
                act.wait_ge(s["w1_in"], 16 * (e + 1))
                act.wait_ge(s["h_psum"], FC * e)
                nc.scalar.activation(w1hi[:, :, cols], w1raw[:, :, cols], ACT.Copy
                                     ).then_inc(s["w1hi_done"], 1)

            act.wait_ge(s["a_done"], 2)
            for g in range(HALVES * DS):
                if g == 0:
                    b_copies(0)
                decay(g)
                b_copies(g + (1 if g == 1 else 2))
                if g == HALVES * DS - 2:
                    z_silu(range(HTILES, TILES))
                if g == SILU:
                    conv_silu(1)
                    b_copies(g + 3)
                    z_silu(range(2, HTILES))
                    b_copies(g + 4)
                n = g - RING
                if n == PROJ:
                    parts(1)
                if n in (DELTA, DELTA + 1):
                    exps(1, n - DELTA)
                if n == DELTA + 1:
                    b_copies(g + 3)
                    logs(1)
                    b_copies(g + 4)
                if n in (ZTURN, ZTURN + 1):
                    z_turned(n - ZTURN)
                n -= DS
                if n in (TURN, TURN + 1):
                    x1_turned(0, n - TURN)
                if n in (LOGIT, LOGIT + 1):
                    logits_out(0, n - LOGIT)
                if n == COUNT:
                    counts_out(0)
                if LOGIT + 2 <= n < LOGIT + 2 + HTILES:
                    normalise(n - LOGIT - 2)
                if n == COUNT:
                    top_exp(0)
            for m in range(WP):
                split_w1(0, m)
            z_turned(2)
            z_turned(3)
            x1_turned(1, 0)
            x1_turned(1, 1)
            logits_out(1, 0)
            logits_out(1, 1)
            top_exp(1)
            counts_out(1)
            for j in range(HTILES, TILES):
                normalise(j)

            def split_w2(e, m):
                fs = slice(m * FP, (m + 1) * FP)
                act.wait_ge(s["w2_in"], 16 * (e + 1))
                act.wait_ge(s["o_psum"], e)
                nc.scalar.activation(w2hi[:, fs, :], w2raw[:, fs, :], ACT.Copy).then_inc(s["w2hi_done"], 1)

            def rows_hi(e):
                act.wait_ge(s["xet_psum"], e + KC)
                nc.scalar.activation(xthi[:, :, bass.ds(e * CAP, CAP)], ps[:, 6:8, 0:CAP], ACT.Copy
                                     ).then_inc(s["xthi_done"], 1)

            def hidden_hi(e, f):
                act.wait_ge(s["h_psum"], e * FC + f + 1)
                nc.scalar.activation(hthi[:, f, :], ps[:, f % 4, 0:CAP], ACT.Relu).then_inc(s["hthi_done"], 1)

            def expert(e, first, last):
                for f in range(FC):
                    hidden_hi(e, f)
                    if f < WP:
                        split_w2(e, f)
                if not last:
                    rows_hi(e + 1)
                    for m in range(WP):
                        split_w1(e + 1, m)
                if last:
                    for c in range(KC):
                        act.wait_ge(s["o_psum"], NE + c)
                        nc.scalar.activation(eot[:, c, :], ps[:, 4 + c, 0:CAP], ACT.Copy
                                             ).then_inc(s["o_done"], 1)
                else:
                    act.wait_ge(s["o_psum"], e + 1)
                    nc.scalar.activation(eot[:], ps[:, 4:6, 0:CAP], ACT.Copy).then_inc(s["o_done"], 1)

            for c in range(KC):
                act.wait_ge(s["xet_psum"], c + 1)
                nc.scalar.activation(xthi[:, c, 0:CAP], ps[:, 6 + c, 0:CAP], ACT.Copy
                                     ).then_inc(s["xthi_done"], 1)
            expert(0, True, False)
            with act.Fori(1, NE - 1) as e:
                expert(e, False, False)
            expert(NE - 1, False, True)

        @block.tensor
        def _(pe):
            pe.sem_inc(s["ysum_done"], SUMS)
            pe.wait_ge(s["fill_made"], 1)

            def keep_clock(n, bank):
                for _ in range(n):
                    nc.tensor.matmul(ps[:, bank, 0:P], onesf[:], onesf[:], start=True, stop=True)

            keep_clock(11, BBANK + 1)

            def conv(hb, c):
                acc = ps[:, WORK + c, :].rearrange("p (b l) -> p b l", b=HB)
                src = ctxs[:, halves(hb)].rearrange("p (b l) -> p b l", b=HB)
                for k in range(TAPS):
                    ins = nc.tensor.matmul(acc[:, :, k:L], cwb[:, TAPS - 1 - k, c * P:(c + 1) * P],
                                           src[:, :, 0:L - k], start=(k == 0), stop=(k == TAPS - 1),
                                           skip_group_check=True)
                ins.then_inc(s["conv_psum"], 1)

            def x_proj(hb):
                pe.wait_ge(s["u_done"], EC * (hb + 1))
                for c in range(EC):
                    ins = nc.tensor.matmul(ps[0:XPC, PBANK[hb], :], xps[:, c, :], u[:, c, halves(hb)],
                                           start=(c == 0), stop=(c == EC - 1))
                ins.then_inc(s["xp_psum"], 1)

            def dt_proj(hb, c):
                pe.wait_ge(s["dtlo_done"], hb + 1)
                nc.tensor.matmul(ps[:, DBANK[hb * EC + c], :], dtps[3 * BC:3 * BC + DR, c * P:(c + 1) * P],
                                 dtlo[3 * BC:3 * BC + DR, halves(hb)], start=True, stop=True
                                 ).then_inc(s["dt_psum"], 1)

            def z_turn(m):
                for n in range(4):
                    j, c = 2 * m + n // 2, n % 2
                    ins = nc.tensor.transpose(
                        ps[:, WORK + m % 2, n * P:(n + 1) * P],
                        zs[:, (j // 2) * 2 + c, (j % 2) * P:(j % 2 + 1) * P], ident)
                ins.then_inc(s["zt_psum"], 1)

            def b_cast(hb, g, n, par):
                if not isinstance(g, int) or g >= SUMS:
                    pe.wait_ge(s["b_done"], g - SUMS + 1)
                nc.tensor.matmul(ps[:, BBANK + par, :], sels[:, bass.ds(n * P, P)], stack[:, halves(hb)],
                                 start=True, stop=True).then_inc(s["b_psum"], 1)

            def c_cast(hb, g, n, par):
                pe.wait_ge(s["mult_done"], RING + g - SUMS + 1)
                nc.tensor.matmul(ps[:, CBANK + par, :], sels[:, bass.ds((DS + n) * P, P)],
                                 stack[:, halves(hb)], start=True, stop=True).then_inc(s["c_psum"], 1)

            def add_state(g, par, tiles, last):
                pe.wait_ge(s["mult_done"], RING + g + 1)
                for t in tiles:
                    for c in range(EC):
                        ins = nc.tensor.matmul(y[:, t, c * P:(c + 1) * P], hc[par][:, c, t * P:(t + 1) * P],
                                               ident, start=False, stop=last, skip_group_check=True)
                return ins

            def state_sum(g, par, last=False):
                add_state(g, par, range(HTILES), last).then_inc(s["ysum_done"], 1)

            def turn_x1(hb, m):
                pe.wait_ge(s["x1_done"], 2 * hb + m + 1)
                for c in range(KC):
                    for t in range(2):
                        ins = nc.tensor.transpose(
                            ps[:, WORK + m, (2 * c + t) * P:(2 * c + t + 1) * P],
                            x1[:, hb * HTILES + 2 * m + t, c * P:(c + 1) * P], ident)
                ins.then_inc(s["xt_psum"], 1)

            def logits(hb, m):
                pe.wait_ge(s["wg_done"], 1)
                pe.wait_ge(s["xt_done"], 2 * hb + m + 1)
                for t in range(2):
                    for c in range(KC):
                        tile = 2 * m + t
                        ins = nc.tensor.matmul(ps[:, WORK + m, t * NE:(t + 1) * NE],
                                               xnt[:, c, tile * P:(tile + 1) * P], wgs[:, c, :],
                                               start=(t == 0 and c == 0), stop=(c == KC - 1),
                                               skip_group_check=True)
                ins.then_inc(s["lg_psum"], 1)

            def counts(hb):
                pe.wait_ge(s["multi_done"], hb + 1)
                before = ps[:, WORK, 0:HTILES * NE].rearrange("p (t e) -> p t e", e=NE)
                mh = multi[:, hb * HTILES:(hb + 1) * HTILES, :]
                last = nc.tensor.matmul(before, tri[:], mh, start=True, stop=False, skip_group_check=True)
                for t in range(1, HTILES):
                    last = nc.tensor.matmul(before[:, t:HTILES, :], ones[:], mh[:, 0:HTILES - t, :],
                                            start=False, stop=False, skip_group_check=True)
                for j in range(hb * HTILES):
                    last = nc.tensor.matmul(before, ones[:], multi[:, j:j + 1, :].to_broadcast([P, HTILES, NE]),
                                            start=False, stop=False, skip_group_check=True)
                last.then_inc(s["pos_psum"], 1)

            pe.wait_ge(s["ctx_in0"], 16)
            pe.wait_ge(s["cw_done"], 1)
            for c in range(EC):
                conv(0, c)
            pe.wait_ge(s["small_in"], 64)
            for c in range(KC):
                ins = nc.tensor.matmul(ps[:, 0, 0:NE], onesf[:], wgs[:, c, :], start=(c == 0),
                                       stop=(c == KC - 1))
            ins.then_inc(s["wg_psum"], 1)
            x_proj(0)
            for c in range(EC):
                dt_proj(0, c)
            def open_sums(hb):
                for t in range(HTILES):
                    for c in range(EC):
                        nc.tensor.matmul(y[:, t, c * P:(c + 1) * P],
                                         u[:, c, hb * HT + t * P:hb * HT + (t + 1) * P], diagd[:, c, :],
                                         start=(t % 2 == 0 and c == 0), stop=False, skip_group_check=True)

            def step(hb, n, par):
                g = hb * DS + n
                for cast, lead in ((c_cast, 1), (b_cast, AHEAD)):
                    if not isinstance(n, int) or n + lead < DS:
                        cast(hb, g + lead, n + lead, (par + lead) % SUMS)
                    elif hb + 1 < HALVES:
                        cast(hb + 1, g + lead, n + lead - DS, (par + lead) % SUMS)
                if not isinstance(n, int) or n > 0 or hb > 0:
                    if isinstance(n, int) and n == 0:
                        state_sum(g - 1, 1 - par, last=True)
                    else:
                        state_sum(g - 1, 1 - par)

            pe.wait_ge(s["sel_in"], 16)
            pe.wait_ge(s["stack_done"], 1)
            b_cast(0, 0, 0, 0)
            b_cast(0, 1, 1, 1)
            c_cast(0, 0, 0, 0)
            pe.wait_ge(s["ctx_in1"], 16)
            pe.wait_ge(s["sp_relu"], 1)
            conv(1, 0)
            b_cast(0, 2, 2, 0)
            pe.wait_ge(s["sp_relu"], EC)
            conv(1, 1)
            pe.wait_ge(s["a_done"], 2)
            pe.wait_ge(s["wg_done"], 1)
            b_cast(0, 3, 3, 1)
            open_sums(0)
            for n in range(4, AHEAD):
                b_cast(0, n, n, n % SUMS)
            for n in range(ZTURN):
                step(0, n, n % 2)
                if n == PROJ:
                    x_proj(1)
                if n in (DELTA, DELTA + 1):
                    if n == DELTA + 1:
                        pe.wait_ge(s["hi_done"], 2)
                    dt_proj(1, n - DELTA)
            pe.wait_ge(s["sp_relu"], EC * HALVES)
            pe.wait_ge(s["zs_done"], 2)
            for n in range(ZTURN, DS):
                if n + AHEAD == DS:
                    pe.wait_ge(s["stack_done"], 2)
                step(0, n, n % 2)
                if n in (ZTURN, ZTURN + 1):
                    z_turn(n - ZTURN)
            step(1, 0, 0)
            c_cast(1, DS + 2, 2, 0)
            b_cast(1, DS + 1 + AHEAD, 1 + AHEAD, (1 + AHEAD) % SUMS)
            pe.wait_ge(s["y_used"], 1)
            open_sums(1)
            state_sum(DS, 0)

            def route(n):
                if n in (TURN, TURN + 1):
                    pe.wait_ge(s["zt_done"], 2)
                    turn_x1(0, n - TURN)
                if n in (LOGIT, LOGIT + 1):
                    logits(0, n - LOGIT)
                if n == COUNT:
                    pe.wait_ge(s["lg_done"], 2)
                    counts(0)

            for n in range(2, 6):
                step(1, n, n % 2)
                route(n)
            with pe.Fori(3, 4) as i:
                for par in range(2):
                    step(1, 2 * i + par, par)
            for n in range(8, DS):
                step(1, n, n % 2)
                if n == COUNT:
                    route(n)
                if n == DS - 4:
                    pe.wait_ge(s["pos_done"], 1)
                    keep_clock(4, WORK)
                if n == DS - 3:
                    pe.wait_ge(s["zs_done"], 3)
                    z_turn(2)
                    z_turn(3)
            add_state(2 * DS - 1, 1, range(2), True).then_inc(s["y_half"], 1)
            add_state(2 * DS - 1, 1, range(2, HTILES), True).then_inc(s["ysum_done"], 1)
            pe.wait_ge(s["zt_done"], 4)
            keep_clock(3, WORK)
            turn_x1(1, 0)
            keep_clock(3, WORK + 1)
            turn_x1(1, 1)
            logits(1, 0)
            logits(1, 1)
            pe.wait_ge(s["b_done"], HALVES * DS)
            pe.wait_ge(s["xe_in"], 32)
            for c in range(KC):
                for t in range(ET):
                    nc.tensor.matmul(ps[:, 6 + c, t * P:t * P + EROWS[t]],
                                     xe[0:EROWS[t], t, c * P:(c + 1) * P],
                                     cst[0:EROWS[t], CID:CID + EROWS[t]], start=(t == 0), stop=False,
                                     skip_group_check=True)

            keep_clock(2, CBANK + 1)
            pe.wait_ge(s["lg_done"], 4)
            counts(1)
            keep_clock(8, CBANK + 1)
            pe.wait_ge(s["pos_done"], 2)

            def split_mm(out_, hi_a, lo_a, hi_b, lo_b, start, stop):
                nc.tensor.matmul(out_, hi_a, hi_b, start=start, stop=False)
                nc.tensor.matmul(out_, hi_a, lo_b, start=False, stop=False)
                return nc.tensor.matmul(out_, lo_a, hi_b, start=False, stop=stop)

            def turn_rows(e):
                pe.wait_ge(s["xe_in"], 32 * (e + 1))
                for c in range(KC):
                    for t in range(ET):
                        ins = nc.tensor.transpose(ps[:, 6 + c, t * P:t * P + EROWS[t]],
                                                  xe[0:EROWS[t], t, c * P:(c + 1) * P],
                                                  cst[0:EROWS[t], CID:CID + EROWS[t]])
                ins.then_inc(s["xet_psum"], 1)

            def turn_results(e, chunks=range(KC)):
                for t in range(ET):
                    for c in chunks:
                        ins = nc.tensor.transpose(
                            ps[0:EROWS[t], 6 + t // 2, (t % 2) * DM + c * P:(t % 2) * DM + (c + 1) * P],
                            eot[:, c, t * P:t * P + EROWS[t]], ident)
                return ins

            def expert(e, first, last):
                slots = bass.ds(e * CAP, CAP)

                def hidden_part(f, c):
                    fs = slice(f * P, (f + 1) * P)
                    return split_mm(ps[:, f % 4, 0:CAP], w1hi[:, c, fs], w1lo[:, c, fs],
                                    xthi[:, c, slots], xtlo[:, c, slots], c == 0, c == KC - 1)

                if first:
                    for c in range(KC):
                        pe.wait_ge(s["xthi_done"], c + 1)
                        pe.wait_ge(s["xtlo_done"], c + 1)
                        for f in range(4):
                            if c == 0 and f % FP == 0:
                                pe.wait_ge(s["w1lo_done"], f // FP + 1)
                            ins = hidden_part(f, c)
                            if c == KC - 1:
                                ins.then_inc(s["h_psum"], 1)
                else:
                    pe.wait_ge(s["xthi_done"], e + KC)
                    pe.wait_ge(s["xtlo_done"], e + KC)
                for f in range(4 if first else 0, FC):
                    if f % FP == 0:
                        pe.wait_ge(s["w1hi_done"], WP * e + f // FP + 1)
                        pe.wait_ge(s["w1lo_done"], WP * e + f // FP + 1)
                    if f >= 4:
                        pe.wait_ge(s["htlo_done"], e * FC + f - 3)
                    for c in range(KC):
                        ins = hidden_part(f, c)
                    ins.then_inc(s["h_psum"], 1)
                    if f == 1 and not first:
                        pe.wait_ge(s["o_done"], e)
                        turn_results(e - 1).then_inc(s["r_psum"], 1)
                if not last and not first:
                    pe.wait_ge(s["r_done"], ET * e)
                    turn_rows(e + 1)

                def out_part(f, c):
                    cs = slice(c * P, (c + 1) * P)
                    return split_mm(ps[:, 4 + c, 0:CAP], w2hi[:, f, cs], w2lo[:, f, cs],
                                    hthi[:, f, :], htlo[:, f, :], f == 0, f == FC - 1)

                for c in range(KC if last else 1):
                    for f in range(FC):
                        if first and f == 4:
                            turn_rows(1)
                        if f % FP == 0:
                            pe.wait_ge(s["w2hi_done"], WP * e + f // FP + 1)
                            pe.wait_ge(s["w2lo_done"], WP * e + f // FP + 1)
                        pe.wait_ge(s["htlo_done"], e * FC + f + 1)
                        if last:
                            ins = out_part(f, c)
                        else:
                            for cc in range(KC):
                                ins = out_part(f, cc)
                    ins.then_inc(s["o_psum"], 1)

            for c in range(KC):
                for t in range(HTILES):
                    pe.wait_ge(s["takes_done"], t + 1)
                    pe.wait_ge(s["xn_done"], HTILES + t + 1)
                    ins = nc.tensor.matmul(ps[:, 6 + c, 0:CAP], xrow[:, HTILES + t, 0, c * P:(c + 1) * P],
                                           takes[:, t, :], start=False, stop=(t == HTILES - 1),
                                           skip_group_check=True)
                ins.then_inc(s["xet_psum"], 1)
            expert(0, True, False)
            with pe.Fori(1, NE - 1) as e:
                expert(e, False, False)
            expert(NE - 1, False, True)
            pe.wait_ge(s["r_done"], ET * (NE - 1))
            for c in range(KC):
                pe.wait_ge(s["o_done"], NE + c)
                ins = turn_results(NE - 1, [c])
            ins.then_inc(s["r_psum"], 1)

        @block.vector
        def _(dve):
            linked = [0]

            def link(ins):
                linked[0] += 1
                ins.then_inc(s["dve_step"], 1)
                dve.wait_ge(s["dve_step"], linked[0])

            dve.wait_ge(s["inp_in"], 16)
            dve.wait_ge(s["cw_in"], 16)
            nc.vector.tensor_tensor(cwb, cwb, inps[:, None, :].to_broadcast([P, TAPS, DI]), ALU.mult
                                    ).then_inc(s["cw_done"], 1)
            dve.sem_inc(s["mult_done"], RING)
            for r in range(RING):
                nc.vector.memset(da[r][:].rearrange("p c (b l) -> p (c b) l", l=L)[:, :, 0:1], 0.0
                                 ).then_inc(s["scan_done"], 1)
            dve.wait_ge(s["x_in"], 16)
            for j in range(TILES):
                ins = nc.vector.bn_stats(stats[:, j, :], xnat[:, j, :])
            link(ins)
            for j in range(TILES):
                ins = nc.vector.bn_aggr(mvz[:, j, :], stats[:, j, :])
            link(ins)
            nc.vector.tensor_scalar(vz[:], mvz[:, :, 1], EPS, None, ALU.add).then_inc(s["z_stats"], 1)
            dve.wait_ge(s["z_rstd"], 1)
            nc.vector.scalar_tensor_tensor(out=nmz[:], in0=mvz[:, :, 0], scalar=-1.0, in1=rz[:],
                                           op0=ALU.mult, op1=ALU.mult).then_inc(s["z_scale"], 1)
            dve.wait_ge(s["wg_psum"], 1)
            nc.vector.scalar_tensor_tensor(
                out=wgs[:], in0=ps[:, 0:1, 0:NE].to_broadcast([P, KC, NE]), scalar=-1.0 / DM, in1=wgs[:],
                op0=ALU.mult, op1=ALU.add).then_inc(s["wg_done"], 1)

            def parts(hb):
                cols = halves(hb)
                dve.wait_ge(s["hi_done"], hb + 1)
                bc = rest[:] if hb else ps[0:3 * BC, PBANK[hb], :]
                link(nc.vector.tensor_tensor(rest[:], bc, stack[:, cols], ALU.subtract))
                nc.vector.tensor_copy(stack[BC:2 * BC, cols], rest[BC:2 * BC, :])
                link(nc.vector.tensor_copy(stack[2 * BC:3 * BC, cols], rest[2 * BC:3 * BC, :]))
                nc.vector.tensor_tensor(stack[2 * BC:3 * BC, cols], rest[2 * BC:3 * BC, :],
                                        stack[2 * BC:3 * BC, cols], ALU.subtract
                                        ).then_inc(s["stack_done"], 1)

            def softplus(hb):
                for c in range(EC):
                    dve.wait_ge(s["sp_exp"], hb * EC + c + 1)
                    ins = nc.vector.tensor_scalar(delta[:, c, halves(hb)], spe[hb][:, c, :], 1.0, -1.0,
                                                  ALU.add, ALU.add)
                link(ins)
                for c in range(EC):
                    d = delta[:, c, halves(hb)]
                    dve.wait_ge(s["sp_sum"], hb * EC + c + 1)
                    ins = nc.vector.tensor_tensor(d, spr[hb][:, c, :], d, ALU.subtract)
                link(ins)
                for c in range(EC):
                    d = delta[:, c, halves(hb)]
                    dve.wait_ge(s["sp_ln"], hb * EC + c + 1)
                    nc.vector.tensor_tensor(d, spl[hb][:, c, :], d, ALU.add).then_inc(s["delta_done"], 1)

            dve.wait_ge(s["ch_in"], 16)
            dve.wait_ge(s["small_in"], 64)
            parts(0)
            for c in range(EC):
                dve.wait_ge(s["sp_abs"], c + 1)
                nc.vector.tensor_scalar(spr[0][:, c, :], ps[:, DBANK[c], :], ch[:, c, DTB:DTB + 1], 0.0,
                                        ALU.add, ALU.max).then_inc(s["sp_relu"], 1)
            for c in range(EC):
                ins = nc.vector.tensor_scalar(diagd[:, c, :], ident, ch[:, c, DSK:DSK + 1], None, ALU.mult)
            ins.then_inc(s["a_done"], 1)
            nc.vector.tensor_copy(tri[:], cst[:, CTRI:CTRI + P])
            for j in range(TILES):
                nc.vector.tensor_copy(xrow[:, j, :, DM + 1], cst[:, CDST + j:CDST + j + 1].to_broadcast([P, TOPK]))
            dve.wait_ge(s["a_exp"], 1)
            nc.vector.tensor_scalar(anegs[:], anegs[:], -1.0, None, ALU.mult).then_inc(s["a_done"], 1)
            softplus(0)
            def scan(g, r):
                dve.wait_ge(s["mult_done"], g + 1)
                dve.wait_ge(s["da_done"], EC * (g + 1))
                dve.wait_ge(s["dbu_done"], g + RING + 1)
                nc.vector.tensor_tensor_scan(h[r][:].rearrange("p c t -> p (c t)"),
                                             da[r][:].rearrange("p c t -> p (c t)"),
                                             dbu[r][:].rearrange("p c t -> p (c t)"), 0.0,
                                             ALU.mult, ALU.add).then_inc(s["scan_done"], 1)

            def mult(g, r):
                dve.wait_ge(s["scan_done"], g + RING + 1)
                dve.wait_ge(s["c_psum"], g + 1)
                dve.wait_ge(s["ysum_done"], g + 1)
                bank = CBANK + r % SUMS
                nc.vector.tensor_tensor(hc[r % SUMS][:], h[r][:],
                                        ps[:, bank:bank + 1, :].to_broadcast([P, EC, HT]),
                                        ALU.mult).then_inc(s["mult_done"], 1)

            def step(g, r):
                scan(g + 1, (r + 1) % RING)
                mult(g, r)

            def steps(lo, hi):
                with dve.Fori(lo, hi) as i:
                    for r in range(RING):
                        step(RING * i + r, r)

            def gate_y(hb, m):
                tiles = slice(hb * HTILES + 2 * m, hb * HTILES + 2 * m + 2)
                return nc.vector.tensor_tensor(x1[:, tiles, :], y[:, 2 * m:2 * m + 2, :], zst[:, tiles, :],
                                               ALU.mult)

            def add_x(hb, m):
                tiles = slice(hb * HTILES + 2 * m, hb * HTILES + 2 * m + 2)
                nc.vector.tensor_tensor(x1[:, tiles, :], x1[:, tiles, :], xnat[:, tiles, :], ALU.add
                                        ).then_inc(s["x1_done"], 1)

            def row_stats(hb, m):
                dve.wait_ge(s["x1_done"], 2 * hb + m + 1)
                for j in range(hb * HTILES + 2 * m, hb * HTILES + 2 * m + 2):
                    ins = nc.vector.bn_stats(stats[:, j, :], x1[:, j, :])
                return ins

            def variance(hb, ins):
                tiles = slice(hb * HTILES, (hb + 1) * HTILES)
                link(ins)
                for j in range(hb * HTILES, (hb + 1) * HTILES):
                    ins = nc.vector.bn_aggr(mvx[:, j, :], stats[:, j, :])
                link(ins)
                nc.vector.tensor_scalar(vx[:, tiles], mvx[:, tiles, 1], EPS, None, ALU.add
                                        ).then_inc(s["ln_var"], 1)

            def choose(hb):
                tiles = slice(hb * HTILES, (hb + 1) * HTILES)
                js = range(hb * HTILES, (hb + 1) * HTILES)
                dve.wait_ge(s["lg_done"], 2 * hb + 2)
                for j in js:
                    ins = nc.vector.max(top[:, j, :], lg[:, j, :])
                link(ins)
                for j in js:
                    ins = nc.vector.max_index(topi[:, j, :], top[:, j, :], lg[:, j, :])
                link(ins)
                link(nc.vector.tensor_copy(topf[:, tiles, :], topi[:, tiles, 0:TOPK]))
                link(nc.vector.tensor_tensor(
                    oh[:, tiles, :, :],
                    cst[:, None, None, CIOTA:CIOTA + NE].to_broadcast([P, HTILES, TOPK, NE]),
                    topf[:, tiles, :, None].to_broadcast([P, HTILES, TOPK, NE]), ALU.is_equal))
                nc.vector.tensor_tensor(multi[:, tiles, :], oh[:, tiles, 0, :], oh[:, tiles, 1, :], ALU.add
                                        ).then_inc(s["multi_done"], 1)
                link(nc.vector.tensor_tensor(etop[:, tiles, :], top[:, tiles, :],
                                             top[:, tiles, 0:1].to_broadcast([P, HTILES, NE]),
                                             ALU.subtract))
                dve.wait_ge(s["ln_rstd"], hb + 1)
                nc.vector.tensor_tensor(etop[:, tiles, :], etop[:, tiles, :],
                                        rx[:, tiles, None].to_broadcast([P, HTILES, NE]), ALU.mult
                                        ).then_inc(s["top_sub"], 1)
                nc.vector.scalar_tensor_tensor(out=nmx[:, tiles], in0=mvx[:, tiles, 0], scalar=-1.0,
                                               in1=rx[:, tiles], op0=ALU.mult, op1=ALU.mult
                                               ).then_inc(s["ln_scale"], 1)

            def place(hb):
                tiles = slice(hb * HTILES, (hb + 1) * HTILES)
                dve.wait_ge(s["top_exp"], hb + 1)
                link(nc.vector.tensor_reduce(rsum[:, tiles], etop[:, tiles, :], AX.X, ALU.add))
                link(nc.vector.reciprocal(rsum[:, tiles], rsum[:, tiles]))
                nc.vector.tensor_tensor(xrow[:, tiles, :, DM], etop[:, tiles, 0:TOPK],
                                        rsum[:, tiles, None].to_broadcast([P, HTILES, TOPK]), ALU.mult
                                        ).then_inc(s["gates_done"], 1)
                dve.wait_ge(s["pos_done"], hb + 1)
                link(nc.vector.tensor_tensor(ohc[:, tiles, :, :], oh[:, tiles, :, :],
                                             cum[:, :, None, :].to_broadcast([P, HTILES, TOPK, NE]), ALU.mult))
                link(nc.vector.tensor_reduce(pos[:, tiles, :], ohc[:, tiles, :, :], AX.X, ALU.add))
                link(nc.vector.scalar_tensor_tensor(out=slot[:, tiles, :], in0=topf[:, tiles, :],
                                                    scalar=float(CAP), in1=pos[:, tiles, :],
                                                    op0=ALU.mult, op1=ALU.add))
                link(nc.vector.tensor_scalar(pos[:, tiles, :], pos[:, tiles, :], float(CAP), DROPPED,
                                             ALU.is_ge, ALU.mult))
                link(nc.vector.tensor_tensor(slot[:, tiles, :], slot[:, tiles, :], pos[:, tiles, :], ALU.add))
                nc.vector.tensor_copy(sloti[:, tiles, :], slot[:, tiles, :]).then_inc(s["slots_done"], 1)

            def low_w1(e, m):
                cols = slice(m * FP * P, (m + 1) * FP * P)
                dve.wait_ge(s["w1hi_done"], WP * e + m + 1)
                nc.vector.tensor_tensor(w1lo[:, :, cols], w1raw[:, :, cols], w1hi[:, :, cols].bitcast(F32),
                                        ALU.subtract).then_inc(s["w1lo_done"], 1)

            dve.wait_ge(s["delta_done"], EC)
            nc.vector.tensor_tensor(du[:, 1, halves(0)], delta[:, 1, halves(0)], u[:, 1, halves(0)],
                                    ALU.mult).then_inc(s["du_done"], 1)
            dve.wait_ge(s["du_done"], EC)
            for g in range(2):
                dve.wait_ge(s["b_done"], g + 1)
                nc.vector.tensor_tensor(dbu[g][:], du[:, :, halves(0)],
                                        bsb[g][:, None, :].to_broadcast([P, EC, HT]), ALU.mult
                                        ).then_inc(s["first_dbu"], 1)
                dve.wait_ge(s["first_dbu"], g + 1)
                scan(g, g)
            mult(0, 0)
            for r in range(1, RING):
                step(r, r)
            steps(1, 2)
            parts(1)
            for g in range(2 * RING, 11):
                step(g, g % RING)
            softplus(1)
            for g in range(11, 3 * RING):
                step(g, g % RING)
            steps(3, 4)
            step(DS, 0)
            dve.wait_ge(s["ysum_done"], DS + SUMS)
            dve.wait_ge(s["zt_done"], 2)
            gate_y(0, 0)
            gate_y(0, 1).then_inc(s["y_used"], 1)
            step(DS + 1, 1)
            dve.wait_ge(s["y_used"], 1)
            add_x(0, 0)
            add_x(0, 1)
            step(DS + 2, 2)
            row_stats(0, 0)
            variance(0, row_stats(0, 1))
            step(DS + 3, 3)
            steps(5, 6)
            choose(0)
            steps(6, 7)
            place(0)
            for r in range(RING - 1):
                step(2 * DS - RING + r, r)
            mult(2 * DS - 1, RING - 1)
            dve.wait_ge(s["zt_done"], 4)
            dve.wait_ge(s["y_half"], 1)
            gate_y(1, 0).then_inc(s["y_used"], 1)
            dve.wait_ge(s["ysum_done"], HALVES * DS + SUMS)
            gate_y(1, 1).then_inc(s["y_used"], 1)
            for m in range(2):
                dve.wait_ge(s["y_used"], m + 2)
                add_x(1, m)
            row_stats(1, 0)
            variance(1, row_stats(1, 1))
            choose(1)
            place(1)

            def metas(e, first):
                if first:
                    dve.wait_ge(s["meta_in"], 32)
                else:
                    dve.wait_ge(s["xe_in"], 32 * (e + 1))
                for t0, t1, rows in ((0, 2, P), (2, 3, EROWS[2])):
                    tiles = bass.ds(e * ET + t0, t1 - t0)
                    two = meta0[0:rows, t0:t1, :] if first else xe[0:rows, t0:t1, DM:ROW]
                    nc.vector.tensor_copy(gates[0:rows, tiles, :], two[:, :, 0:1])
                    nc.vector.tensor_copy(dst[0:rows, tiles, :], two[:, :, 1:2]
                                          ).then_inc(s["meta_done"], 1)

            def rows_lo(e):
                slots = bass.ds(e * CAP, CAP)
                dve.wait_ge(s["xthi_done"], e + KC)
                nc.vector.tensor_tensor(xtlo[:, :, slots], ps[:, 6:8, 0:CAP], xthi[:, :, slots].bitcast(F32),
                                        ALU.subtract).then_inc(s["xtlo_done"], 1)

            def hidden_lo(e, f):
                dve.wait_ge(s["hthi_done"], e * FC + f + 1)
                nc.vector.scalar_tensor_tensor(out=htlo[:, f, :], in0=ps[:, f % 4, 0:CAP], scalar=0.0,
                                               in1=hthi[:, f, :].bitcast(F32), op0=ALU.max,
                                               op1=ALU.subtract).then_inc(s["htlo_done"], 1)

            def gated_rows(e):
                dve.wait_ge(s["r_psum"], e + 1)
                for t in range(ET):
                    dve.wait_ge(s[f"so_far_in{t}"], 16 * (e + 1))
                    rows = slice(0, EROWS[t])
                    nc.vector.scalar_tensor_tensor(
                        out=eo[rows, t, :], in0=ps[rows, 6 + t // 2, (t % 2) * DM:(t % 2 + 1) * DM],
                        scalar=gates[rows, bass.ds(e * ET + t, 1), 0], in1=so_far[rows, t, :],
                        op0=ALU.mult, op1=ALU.add).then_inc(s["r_done"], 1)

            def expert(e, first, last):
                for f in range(FC):
                    hidden_lo(e, f)
                    if f == 3 and not first:
                        gated_rows(e - 1)
                    if last and f in (5, 6):
                        m = WP // 2 + f - 5
                        fs = slice(m * FP, (m + 1) * FP)
                        dve.wait_ge(s["w2hi_done"], WP * e + m + 1)
                        dve.wait_ge(s["w2lo_done"], WP * e + m)
                        nc.vector.tensor_tensor(w2lo[:, fs, :], w2raw[:, fs, :], w2hi[:, fs, :].bitcast(F32),
                                                ALU.subtract).then_inc(s["w2lo_done"], 1)
                if first:
                    metas(0, True)
                if not last:
                    metas(e + 1, False)
                    rows_lo(e + 1)
                    for m in range(WP):
                        low_w1(e + 1, m)

            tiles = slice(HTILES, TILES)
            link(nc.vector.tensor_tensor(key[:], slot[:, tiles, 0], slot[:, tiles, 1], ALU.min))
            dve.wait_ge(s["numbers_in"], 16)
            for t in range(HTILES):
                nc.vector.tensor_scalar(takes[:, t, :], numbers[:], key[:, t:t + 1], None, ALU.is_equal
                                        ).then_inc(s["takes_done"], 1)
            for m in range(WP):
                low_w1(0, m)
            for c in range(KC):
                dve.wait_ge(s["xthi_done"], c + 1)
                nc.vector.tensor_tensor(xtlo[:, c, 0:CAP], ps[:, 6 + c, 0:CAP], xthi[:, c, 0:CAP].bitcast(F32),
                                        ALU.subtract).then_inc(s["xtlo_done"], 1)
            expert(0, True, False)
            with dve.Fori(1, NE - 1) as e:
                expert(e, False, False)
            expert(NE - 1, False, True)
            gated_rows(NE - 1)


def kernel(x, ctx_1024, L0_xattn_in_proj_w, L0_xattn_conv_w, L0_xattn_conv_b, L0_xattn_x_proj_w,
           L0_xattn_dt_proj_w, L0_xattn_dt_proj_b, L0_xattn_A_log, L0_xattn_D, L0_ffn_Wg, L0_ffn_w1,
           L0_ffn_w2):
    import ml_dtypes
    from concourse import bacc
    from concourse.bass_utils import run_bass_kernel_spmd

    def by_chunk(a):
        a = np.asarray(a)
        return a.reshape(a.shape[0] // P, P, -1).transpose(1, 0, 2)

    x_proj = np.asarray(L0_xattn_x_proj_w).T
    chan = np.concatenate([np.asarray(a).reshape(DI, -1) for a in (
        L0_xattn_conv_b, L0_xattn_dt_proj_b, L0_xattn_D, L0_xattn_A_log)], axis=1)
    consts = np.zeros((P, NCONST), np.float32)
    consts[:, CID:CID + P] = np.eye(P)
    consts[:, CTRI:CTRI + P] = np.triu(np.ones((P, P)), 1)
    for j in range(TILES):
        consts[:, CDST + j] = j * P + np.arange(P)
    consts[:, CIOTA:CIOTA + NE] = np.arange(NE)
    sel = np.zeros((3, BC, BC, P), ml_dtypes.bfloat16)
    for n in range(BC):
        sel[:, n, n, :] = 1.0

    arrays = {
        "x": by_chunk(np.asarray(x).reshape(T, DM)),
        "ctx_t": np.asarray(ctx_1024).reshape(T, DC).T,
        "inproj_t": np.asarray(L0_xattn_in_proj_w).T,
        "xproj_t": by_chunk(np.concatenate([x_proj[:, DR:]] * 3 + [x_proj[:, 0:DR]], axis=1)),
        "dtproj_t": np.asarray(L0_xattn_dt_proj_w).T,
        "conv_w": np.asarray(L0_xattn_conv_w).reshape(DI, TAPS).T,
        "chan": by_chunk(chan),
        "wg": by_chunk(L0_ffn_Wg),
        "w1": np.asarray(L0_ffn_w1).reshape(NE, KC, P, DFF).transpose(0, 2, 1, 3),
        "w2": np.asarray(L0_ffn_w2).reshape(NE, FC, P, DM).transpose(0, 2, 1, 3),
        "consts": consts,
        "slot_numbers": np.broadcast_to(np.arange(CAP, dtype=np.float32), (P, CAP)),
        "sel": sel.reshape(3 * BC, BC * P),
    }
    nc = bacc.Bacc("TRN2", target_bir_lowering=False, num_devices=1)
    ins, feed = {}, {}
    for name, a in arrays.items():
        a = np.ascontiguousarray(a)
        feed["in_" + name] = a
        ins[name] = nc.dram_tensor("in_" + name, a.shape, mybir.dt.from_np(a.dtype), kind="ExternalInput").ap()
    out = nc.dram_tensor("out", [T, DM], F32, kind="ExternalOutput").ap()
    build(nc, out=out, **ins)
    r = run_bass_kernel_spmd(nc, [feed], core_ids=[0])
    return r.results[0]["out"].reshape(B, L, DM)
```
